# Optimizing a Trainium2 kernel written in Bass

```python
import numpy as np
import jax
import jax.numpy as jnp

def _softmax(x, axis=-1):
    return jax.nn.softmax(x, axis=axis)

def _gelu(x):
    return jax.nn.gelu(x, approximate=True)

def _silu(x):
    return jax.nn.silu(x)

def _sigmoid(x):
    return jax.nn.sigmoid(x)

def _layernorm(x, axis=-1, eps=1e-05):
    m = jnp.mean(x, axis=axis, keepdims=True)
    v = jnp.var(x, axis=axis, keepdims=True)
    return (x - m) / jnp.sqrt(v + eps)

def _scatter_add(tgt, idx, src, axis=0):
    return tgt.at[idx].add(src)

def _segment_sum(src, seg, n):
    return jax.ops.segment_sum(src, seg, n)
kernel_name = 'mk_prb_d1_jaxref_r4_b90430'

def setup_inputs(seed: int=0):
    np.random.seed(seed)
    _w = jnp.asarray

    def _L0_attn_setup():
        import jax, jax.numpy as jnp
        import numpy as np
        B, S, D, H = (4, 512, 256, 16)
        DH = D // H
        key = jax.random.key(seed)
        ks = jax.random.split(key, 9)
        sc = 0.02
        return {'x': jax.random.normal(ks[0], (B, S, D), jnp.float32), 'WQ': jax.random.normal(ks[1], (D, D), jnp.float32) * sc, 'bQ': jax.random.normal(ks[2], (D,), jnp.float32) * sc, 'WK': jax.random.normal(ks[3], (D, D), jnp.float32) * sc, 'bK': jax.random.normal(ks[4], (D,), jnp.float32) * sc, 'WV': jax.random.normal(ks[5], (D, D), jnp.float32) * sc, 'bV': jax.random.normal(ks[6], (D,), jnp.float32) * sc, 'WO': jax.random.normal(ks[7], (DH, D), jnp.float32) * sc, 'bO': jax.random.normal(ks[8], (D,), jnp.float32) * sc}
    _L0_attn_in = _L0_attn_setup()

    def _L0_ffn_setup():
        import jax, jax.numpy as jnp
        import numpy as np
        LORA_DIM = 16
        LORA_TOKEN_INDEX = 1
        B, S, D, H = (4, 512, 256, 1024)
        key = jax.random.key(seed)
        ks = jax.random.split(key, 6)
        x = jax.random.normal(ks[0], (B, S, D), dtype=jnp.float32)
        W1 = jax.random.normal(ks[1], (H, D), dtype=jnp.float32) * 0.02
        b1 = jnp.zeros((H,), dtype=jnp.float32)
        W2 = jax.random.normal(ks[2], (D, H), dtype=jnp.float32) * 0.02
        b2 = jnp.zeros((D,), dtype=jnp.float32)
        scale = jnp.asarray(0.001, dtype=jnp.float32)
        return {'x': x, 'W1': W1, 'b1': b1, 'W2': W2, 'b2': b2, 'scale': scale}
    _L0_ffn_in = _L0_ffn_setup()
    _d = {'L0_attn_x': _L0_attn_in['x'], 'L0_attn_WQ': _L0_attn_in['WQ'], 'L0_attn_bQ': _L0_attn_in['bQ'], 'L0_attn_WK': _L0_attn_in['WK'], 'L0_attn_bK': _L0_attn_in['bK'], 'L0_attn_WV': _L0_attn_in['WV'], 'L0_attn_bV': _L0_attn_in['bV'], 'L0_attn_WO': _L0_attn_in['WO'], 'L0_attn_bO': _L0_attn_in['bO'], 'L0_ffn_W1': _L0_ffn_in['W1'], 'L0_ffn_b1': _L0_ffn_in['b1'], 'L0_ffn_W2': _L0_ffn_in['W2'], 'L0_ffn_b2': _L0_ffn_in['b2'], 'L0_ffn_scale': _L0_ffn_in['scale']}
    _x0 = _d['L0_attn_x']
    _d['L0_attn_x'] = jax.random.normal(jax.random.fold_in(jax.random.key(seed), 1), (4, 2048, 256), dtype=_x0.dtype)
    del _x0
    return _d

def reference(L0_attn_x, L0_attn_WQ, L0_attn_bQ, L0_attn_WK, L0_attn_bK, L0_attn_WV, L0_attn_bV, L0_attn_WO, L0_attn_bO, L0_ffn_W1, L0_ffn_b1, L0_ffn_W2, L0_ffn_b2, L0_ffn_scale):

    def _L0_attn_ref(x, WQ, bQ, WK, bK, WV, bV, WO, bO):
        import jax, jax.numpy as jnp
        import numpy as np
        B, S, D, H = (4, 512, 256, 16)
        DH = D // H
        b, s, d = x.shape
        h, dh = (H, DH)
        Q = (x @ WQ + bQ).reshape(b, s, h, dh).transpose(0, 2, 1, 3)
        K = (x @ WK + bK).reshape(b, s, h, dh).transpose(0, 2, 1, 3)
        V = (x @ WV + bV).reshape(b, s, h, dh).transpose(0, 2, 1, 3)
        scale = jnp.sqrt(jnp.float32(dh))
        scores = jnp.einsum('bhqd,bhkd->bhqk', Q, K) / scale
        causal = jnp.tril(jnp.ones((s, s), dtype=bool))
        scores = jnp.where(causal, scores, jnp.float32(-100000.0))
        A = jax.nn.softmax(scores, axis=-1)
        Z = jnp.einsum('bhqk,bhkd->bhqd', A, V)
        out = jnp.einsum('bhsd,de->bse', Z, WO) + jnp.float32(h) * bO
        return out

    def _L0_ffn_ref(x, W1, b1, W2, b2, scale):
        import jax, jax.numpy as jnp
        import numpy as np
        LORA_DIM = 16
        LORA_TOKEN_INDEX = 1
        B, S, D, H = (4, 512, 256, 1024)
        Bx, Sx, Dx = x.shape
        Hx = W1.shape[0]
        lt = jax.lax.dynamic_slice_in_dim(x, LORA_TOKEN_INDEX, LORA_DIM, axis=1)
        even = lt[:, ::2, :]
        odd = lt[:, 1::2, :]
        m1 = (even[:, :4, :, None] * odd[:, :4, None, :]).reshape(Bx, Hx, Dx)
        m2 = (even[:, 4:, :, None] * odd[:, 4:, None, :]).reshape(Bx, Dx, Hx)
        h = jnp.einsum('bsd,hd->bsh', x, W1) + scale * jnp.einsum('bsd,bhd->bsh', x, m1) + b1
        h = jax.nn.gelu(h, approximate=False)
        out = jnp.einsum('bsh,oh->bso', h, W2) + scale * jnp.einsum('bsh,boh->bso', h, m2) + b2
        return out
    x = L0_attn_x
    xn = _layernorm(x, axis=-1)
    x = x + _L0_attn_ref(xn, L0_attn_WQ, L0_attn_bQ, L0_attn_WK, L0_attn_bK, L0_attn_WV, L0_attn_bV, L0_attn_WO, L0_attn_bO) + _L0_ffn_ref(xn, L0_ffn_W1, L0_ffn_b1, L0_ffn_W2, L0_ffn_b2, L0_ffn_scale)
    return x

_drawn_inputs = setup_inputs


def setup_inputs(seed=0):
    import zlib

    import numpy as np

    out = dict(_drawn_inputs(seed))
    spreads = {'L0_ffn_b1': (0.0, 0.8), 'L0_ffn_b2': (0.0, 0.318)}
    factors = {'L0_attn_WQ': 8.0,
     'L0_attn_bQ': 8.0,
     'L0_attn_WK': 8.0,
     'L0_attn_bK': 64.0,
     'L0_attn_WV': 8.0,
     'L0_attn_bV': 8.0,
     'L0_attn_WO': 6.253}
    for name, (base, spread) in spreads.items():
        noise = np.random.default_rng([zlib.crc32(name.encode()), seed]).standard_normal(out[name].shape)
        drawn = base * np.exp(spread * noise) if base else spread * noise
        out[name] = jnp.asarray(drawn.astype(out[name].dtype))
    for name, factor in factors.items():
        out[name] = (out[name] * factor).astype(out[name].dtype)
    return out
```

```python
from contextlib import ExitStack

import concourse.bass as bass
from concourse import mybir
from concourse.alu_op_type import AluOpType as ALU

ACT = mybir.ActivationFunctionType
AX = mybir.AxisListType
F32 = mybir.dt.float32
BF16 = mybir.dt.bfloat16

P = 128
B, S, D, H = 4, 2048, 256, 16
DH = D // H
HID = 1024
TOK = B * S
KD = D // P
CH = 512
CB = S // CH
NCH = TOK // CH
TT = CH // P
GH = 4
QUADS = B * H // GH
QB = H // GH
KT = S // P
VW = 32
PARTS = 3
TERMS = [(0, 0), (0, 1), (1, 0), (1, 1), (0, 2), (2, 0)]
KROWS = len(TERMS) * DH
KMAX = KROWS + PARTS
EPS = 1e-5
NEG = -1e30
LORA = 16
RANKS = 4


def late(m, k):
    return not isinstance(m, int) or m >= k


def turns(b, c):
    return b * (CB // 2) + c // 2


class Alone:

    def __init__(self, eng, tick):
        self.eng, self.tick = eng, tick

    def wait_ge(self, sem, value):
        self.eng.wait_ge(sem, value)
        if not isinstance(value, int):
            self.eng.sem_inc(self.tick, 1)


def pipelined(eng, stage_a, stage_b, lag=1):
    for c in range(CB):
        stage_a(0, c)
        if c >= lag:
            stage_b(0, c - lag)
    with eng.Fori(1, B) as b:
        for c in range(CB):
            stage_a(b, c)
            if c >= lag:
                stage_b(b, c - lag)
            else:
                stage_b(b - 1, c - lag + CB)
    for c in range(CB - lag, CB):
        stage_b(B - 1, c)


def project(nc, const, x, WQ, bQ, WK, bK, WV, bV, qk_scr, v_scr, xnT_scr, lt_scr):
    ident = const["ident"]
    with ExitStack() as ctx:
        sb = lambda name, shape, dt=F32: ctx.enter_context(nc.sbuf_tensor(name, shape, dt))
        sem = lambda name: ctx.enter_context(nc.semaphore(name))
        w_sb = sb("w_sb", [P, 3, KD, D])
        b_in = sb("b_in", [P, 2, 2])
        b_sb = sb("b_sb", [P, 2, 2])
        bv_sb = sb("bv_sb", [P, D])
        x_in = sb("x_in", [P, 2, TT, D])
        xn = sb("xn", [P, 2, TT, D])
        xnT = sb("xnT", [P, 2, KD, CH])
        stats = sb("stats", [P, 2, TT, 6])
        mv = sb("mv", [P, 2, TT, 2])
        veps = sb("veps", [P, 2, TT])
        nmean = sb("nmean", [P, 2, TT])
        std = sb("std", [P, 2, TT])
        rstd = sb("rstd", [P, 2, TT])
        qk32 = sb("qk32", [P, 2, 4, CH])
        parts = sb("parts", [P, 2, 4, PARTS, CH], BF16)
        rest = sb("rest", [P, 4, CH])
        vp = sb("vp", [P, 2, TT, H, VW])
        psT = [ctx.enter_context(nc.psum_tensor(f"psT{d}", [P, CH], F32)) for d in range(KD)]
        psQK = [ctx.enter_context(nc.psum_tensor(f"psQK{k}", [P, CH], F32)) for k in range(4)]
        psV = [ctx.enter_context(nc.psum_tensor(f"psV{k}", [P, 2, D], F32)) for k in range(2)]

        w_loaded = sem("w_loaded")
        x_loaded = [sem(f"x_loaded{u}") for u in range(2)]
        const_ready = sem("const_ready")
        bias_ready = sem("bias_ready")
        stat_step = sem("stat_step")
        var_ready = sem("var_ready")
        std_ready = sem("std_ready")
        rstd_ready = sem("rstd_ready")
        xn_ready = sem("xn_ready")
        xT_ready = sem("xT_ready")
        xnT_ready = sem("xnT_ready")
        qk_ready = sem("qk_ready")
        qk_out = sem("qk_out")
        hi_ready = sem("hi_ready")
        split_step = sem("split_step")
        v_ready = sem("v_ready")
        v_out = sem("v_out")
        stored = [sem(f"stored{u}") for u in range(2)]
        STORES = 2 + 4 + QB

        W_DMAS = 3 + 2 + 1

        pool_tick, dve_tick, sp_tick = sem("pool_tick1"), sem("dve_tick1"), sem("sp_tick1")

        with nc.Block() as block:
            @block.sync
            def _(sp):
                sp_alone = Alone(sp, sp_tick)
                for k, w in enumerate((WQ, WK, WV)):
                    sp.dma_start(w_sb[:, k], w.rearrange("(c p) n -> p c n", p=P)).then_inc(w_loaded, 16)
                for k, b in enumerate((bQ, bK)):
                    sp.dma_start(b_in[:, k], b.rearrange("(g p) -> p g", p=P), allow_slow_non_contiguous=True).then_inc(w_loaded, 16)
                sp.dma_start(bv_sb[:, :], bV.rearrange("(a n) -> a n", a=1).broadcast_to([P, D])).then_inc(w_loaded, 16)

                def load(b, c):
                    m = b * CB + c
                    if late(m, 2):
                        sp.wait_ge(xn_ready, m - 1)
                    sp.dma_start(x_in[:, c % 2], x[b, c * CH:(c + 1) * CH, :].rearrange("(t p) d -> p t d", p=P)).then_inc(x_loaded[c % 2], 16)

                def store(b, c):
                    m, u = b * CB + c, c % 2
                    sp.wait_ge(xn_ready, m + 1)
                    sp.dma_start(lt_scr[m], xn[1:1 + LORA, u, 0, :]).then_inc(stored[u], 16)
                    sp.wait_ge(xnT_ready, m + 1)
                    sp.dma_start(xnT_scr[m], xnT[:, u]).then_inc(stored[u], 16)
                    sp_alone.wait_ge(split_step, 12 * (m + 1))
                    for k in range(4):
                        sp.dma_start(qk_scr[k // 2, :, b, P * (k % 2):P * (k % 2 + 1), c * CH:(c + 1) * CH].rearrange("s r t -> r s t"),
                                     parts[:, u, k]).then_inc(stored[u], 16)
                    sp.wait_ge(v_out, 2 * m + 2)
                    for g in range(QB):
                        sp.dma_start(v_scr[b, g, :, c * TT:(c + 1) * TT, :],
                                     vp[:, u, :, GH * g:GH * (g + 1)].rearrange("p t h w -> p t (h w)")).then_inc(stored[u], 16)

                pipelined(sp, load, store, lag=2)
                for u in range(2):
                    sp.wait_ge(stored[u], 16 * STORES * NCH // 2)

            @block.gpsimd
            def _(pool):
                pool_alone = Alone(pool, pool_tick)
                nc.gpsimd.memset(ident[:], 0.0).then_inc(const_ready, 1)
                nc.gpsimd.memset(const["mask"][:], 0.0).then_inc(const_ready, 1)
                nc.gpsimd.memset(vp[:], 0.0).then_inc(const_ready, 1)
                pool.wait_ge(const_ready, 3)
                nc.gpsimd.affine_select(out=ident[:], in_=ident[:], compare_op=ALU.not_equal, fill=1.0, base=0,
                                        pattern=[[-1, P]], channel_multiplier=1).then_inc(const_ready, 1)
                nc.gpsimd.affine_select(out=const["mask"][:, CH - P:CH], in_=const["mask"][:, CH - P:CH], compare_op=ALU.is_ge,
                                        fill=NEG, base=0, pattern=[[-1, P]], channel_multiplier=1).then_inc(const_ready, 1)
                nc.gpsimd.memset(vp[:, :, :, :, DH:DH + 1], 1.0).then_inc(const_ready, 1)

                def norm(b, c):
                    m, u = b * CB + c, c % 2
                    pool_alone.wait_ge(rstd_ready, m + 1)
                    if late(m, 2):
                        pool_alone.wait_ge(xT_ready, m - 1)
                        pool_alone.wait_ge(stored[u], 16 * STORES * turns(b, c))
                    for t in range(TT):
                        ins = nc.gpsimd.tensor_scalar(xn[:, u, t], x_in[:, u, t], nmean[:, u, t:t + 1], rstd[:, u, t:t + 1],
                                                      ALU.add, ALU.mult)
                    ins.then_inc(xn_ready, 1)

                def high(b, c):
                    m, u = b * CB + c, c % 2
                    if late(m, 2):
                        pool_alone.wait_ge(stored[u], 16 * STORES * turns(b, c))
                        pool_alone.wait_ge(split_step, 12 * (m - 1))
                    for k in range(4):
                        pool_alone.wait_ge(qk_out, 4 * m + k + 1)
                        nc.gpsimd.tensor_scalar(parts[:, u, k, 0], qk32[:, u, k], 1.0, 0.0, ALU.mult, ALU.add).then_inc(hi_ready, 1)

                pipelined(pool, norm, high)

            @block.scalar
            def _(act):
                act.wait_ge(w_loaded, 16 * W_DMAS)
                nc.scalar.activation(b_sb[:, 0], b_in[:, 0], ACT.Identity, scale=0.25).then_inc(bias_ready, 1)
                nc.scalar.activation(b_sb[:, 1], b_in[:, 1], ACT.Identity).then_inc(bias_ready, 1)
                act.wait_ge(bias_ready, 2)

                def turn(b, c):
                    m, u = b * CB + c, c % 2
                    act.wait_ge(var_ready, m + 1)
                    nc.scalar.activation(std[:, u], veps[:, u], ACT.Sqrt).then_inc(std_ready, 1)
                    act.wait_ge(xT_ready, m + 1)
                    if late(m, 2):
                        act.wait_ge(v_ready, 2 * (m - 1))
                        act.wait_ge(stored[u], 16 * STORES * turns(b, c))
                    for d in range(KD):
                        ins = nc.scalar.activation(xnT[:, u, d], psT[d][:], ACT.Identity)
                    ins.then_inc(xnT_ready, 1)

                def out(b, c):
                    m, u = b * CB + c, c % 2
                    if late(m, 2):
                        act.wait_ge(split_step, 12 * (m - 1))
                    for k in range(4):
                        act.wait_ge(qk_ready, 4 * m + k + 1)
                        nc.scalar.activation(qk32[:, u, k], psQK[k][:], ACT.Identity, bias=b_sb[:, k // 2, k % 2:k % 2 + 1],
                                             scale=0.25 if k < 2 else 1.0).then_inc(qk_out, 1)

                pipelined(act, turn, out)

            @block.tensor
            def _(pe):
                pe.wait_ge(const_ready, 6)
                pe.wait_ge(w_loaded, 16 * W_DMAS)

                def turn(b, c):
                    m, u = b * CB + c, c % 2
                    pe.wait_ge(xn_ready, m + 1)
                    if late(m, 1):
                        pe.wait_ge(xnT_ready, m)
                    for t in range(TT):
                        for d in range(KD):
                            ins = pe.transpose(psT[d][:, t * P:(t + 1) * P], xn[:, u, t, d * P:(d + 1) * P], ident[:])
                    ins.then_inc(xT_ready, 1)

                def products(b, c):
                    m, u = b * CB + c, c % 2
                    pe.wait_ge(xnT_ready, m + 1)
                    for k in range(4):
                        if late(m, 1):
                            pe.wait_ge(qk_out, 4 * m - 3 + k)
                        for d in range(KD):
                            ins = pe.matmul(psQK[k][:], w_sb[:, k // 2, d, (k % 2) * P:(k % 2 + 1) * P], xnT[:, u, d],
                                            start=d == 0, stop=d == KD - 1)
                        ins.then_inc(qk_ready, 1)
                    for t in range(TT):
                        if t % 2 == 0 and late(m, 1):
                            pe.wait_ge(v_out, 2 * m - 1 + t // 2)
                        for d in range(KD):
                            ins = pe.matmul(psV[t // 2][:, t % 2], xnT[:, u, d, t * P:(t + 1) * P], w_sb[:, 2, d],
                                            start=d == 0, stop=d == KD - 1)
                        if t % 2 == 1:
                            ins.then_inc(v_ready, 1)

                pipelined(pe, turn, products)

            @block.vector
            def _(dve):
                dve_alone = Alone(dve, dve_tick)
                dve.wait_ge(w_loaded, 16 * W_DMAS)
                dve.wait_ge(const_ready, 6)

                def statistics(b, c):
                    m, u = b * CB + c, c % 2
                    dve.wait_ge(x_loaded[u], 16 * (turns(b, c) + 1))
                    for t in range(TT):
                        ins = nc.vector.bn_stats(stats[:, u, t], x_in[:, u, t])
                    ins.then_inc(stat_step, 1)
                    dve_alone.wait_ge(stat_step, 3 * m + 1)
                    for t in range(TT):
                        ins = nc.vector.bn_aggr(mv[:, u, t], stats[:, u, t])
                    ins.then_inc(stat_step, 1)
                    dve.wait_ge(stat_step, 3 * m + 2)
                    if late(m, 2):
                        dve.wait_ge(xn_ready, m - 1)
                    nc.vector.tensor_scalar(veps[:, u], mv[:, u, :, 1], EPS, None, ALU.add).then_inc(var_ready, 1)
                    nc.vector.tensor_scalar(nmean[:, u], mv[:, u, :, 0], -1.0, None, ALU.mult).then_inc(stat_step, 1)
                    dve.wait_ge(std_ready, m + 1)
                    dve.wait_ge(stat_step, 3 * m + 3)
                    nc.vector.reciprocal(rstd[:, u], std[:, u]).then_inc(rstd_ready, 1)

                def split(b, c):
                    m, u = b * CB + c, c % 2
                    for k in range(4):
                        dve.wait_ge(hi_ready, 4 * m + k + 1)
                        nc.vector.tensor_tensor(rest[:, k], qk32[:, u, k], parts[:, u, k, 0], ALU.subtract).then_inc(split_step, 1)
                        dve.wait_ge(split_step, 12 * m + 3 * k + 1)
                        nc.vector.tensor_copy(parts[:, u, k, 1], rest[:, k]).then_inc(split_step, 1)
                        dve.wait_ge(split_step, 12 * m + 3 * k + 2)
                        nc.vector.tensor_tensor(parts[:, u, k, 2], rest[:, k], parts[:, u, k, 1], ALU.subtract).then_inc(split_step, 1)
                    if late(m, 2):
                        dve.wait_ge(stored[u], 16 * STORES * turns(b, c))
                    for k in range(2):
                        dve.wait_ge(v_ready, 2 * m + k + 1)
                        for t in range(2 * k, 2 * k + 2):
                            ins = nc.vector.tensor_tensor(vp[:, u, t, :, 0:DH], psV[k][:, t % 2].rearrange("p (h w) -> p h w", h=H),
                                                          bv_sb[:].rearrange("p (h w) -> p h w", h=H), ALU.add)
                        ins.then_inc(v_out, 1)

                pipelined(dve, statistics, split)


STEPS = [(c, j) for c in range(CB) for j in range(TT * (c + 1))]
FIRST = [STEPS.index((c, 0)) for c in range(CB)] + [len(STEPS)]
NS = len(STEPS)
MAXIMA = [(h, t, kc) for t in range(KT) for h in range(GH) for kc in range(t // TT + 1)]
NM = len(MAXIMA)
RING = 3
M_FROM, M_TO, M_TURN = 5, 37, 38


def width(c, j):
    return CH - max(0, j - TT * c) * P


def ring_jobs(has_prev, has_next):
    jobs = [[] for _ in range(NS)]
    if has_prev:
        jobs[1].append(("z", CB - 1, True))
    for c in range(CB - 1):
        jobs[FIRST[c + 1] + 1].append(("z", c, False))
    if has_next:
        cost = [width(*STEPS[s]) for s in range(M_FROM, M_TO)]
        total, done, given = sum(cost), 0, 0
        for s, w in zip(range(M_FROM, M_TO), cost):
            done += w
            upto = NM * done // total
            jobs[s] += [("max", k) for k in range(given, upto)]
            given = upto
        jobs[M_TURN].append(("turn",))
    return jobs


def ring_base(n):
    if isinstance(n, int) and n == 0:
        return NM + 1
    return (NM + 1 + CB) * n + NM


def uses_to_z(n, c, has_next):
    if c == CB - 1:
        n, c, has_next = n + 1, -1, True
    jobs = [job for step in ring_jobs(True, has_next) for job in step]
    at = 0 if c < 0 else jobs.index(("z", c, False))
    return (NM + 1 + CB) * n + NM + at + 1


def attend(nc, const, qk_scr, v_scr, zn_scr):
    ident, mask = const["ident"], const["mask"]
    with ExitStack() as ctx:
        sb = lambda name, shape, dt=F32: ctx.enter_context(nc.sbuf_tensor(name, shape, dt))
        sem = lambda name: ctx.enter_context(nc.semaphore(name))
        qs = [sb(f"qs{u}", [KMAX, GH, S], BF16) for u in range(2)]
        ks = [sb(f"ks{u}", [KMAX, GH, S], BF16) for u in range(2)]
        vq = [sb(f"vq{u}", [P, KT, GH, VW]) for u in range(2)]
        pr = [[sb(f"pr{p}{v}", [P, 2, CH]) for v in range(2)] for p in range(2)]
        mx = sb("mx", [P, GH, KT, CB])
        negm = sb("negm", [P, P])
        mrest = sb("mrest", [GH * KT, P])
        mparts = sb("mparts", [GH * KT, PARTS, P], BF16)
        zt = [sb(f"zt{v}", [P, CH]) for v in range(2)]
        rl = sb("rl", [P, TT, GH])
        zn = [sb(f"zn{v}", [P, TT, GH, DH]) for v in range(2)]
        sc = [ctx.enter_context(nc.psum_tensor(f"sc{p}", [P, 2, CH], F32)) for p in range(2)]
        ring = [ctx.enter_context(nc.psum_tensor(f"ring{k}", [P, CH], F32)) for k in range(RING)]
        pv = ctx.enter_context(nc.psum_tensor("pv", [P, CH], F32))

        qk_loaded = sem("qk_loaded")
        v_loaded = sem("v_loaded")
        set_up = sem("set_up")
        sc_ready = sem("sc_ready")
        exp_done = sem("exp_done")
        masked = sem("masked")
        pv_done = sem("pv_done")
        zt_done = sem("zt_done")
        ring_ready = sem("ring_ready")
        ring_done = sem("ring_done")
        negm_ready = sem("negm_ready")
        m_step = sem("m_step")
        m_landed = sem("m_landed")
        rl_ready = sem("rl_ready")
        zn_stored = [sem(f"zn_stored{u}") for u in range(2)]
        QKD = 16 * 2 * len(TERMS)
        DIAG = 2 * TT * CB

        def groups(eng, group):
            group(0, 0, False, True)
            with eng.Fori(0, (QUADS - 2) // 2) as i:
                group(2 * i + 1, 1, True, True)
                group(2 * i + 2, 0, True, True)
            group(QUADS - 1, 1, True, False)

        pool_tick, dve_tick, sp_tick = sem("pool_tick2"), sem("dve_tick2"), sem("sp_tick2")

        with nc.Block() as block:
            @block.sync
            def _(sp):
                sp_alone = Alone(sp, sp_tick)
                def load_qk(n, u):
                    for w, dst in ((0, qs[u]), (1, ks[u])):
                        rows = qk_scr[w].rearrange("s b (g h d) t -> s (b g) d h t", g=QB, d=DH)
                        for i, term in enumerate(TERMS):
                            sp.dma_start(dst[DH * i:DH * (i + 1), :, :], rows[term[w], n]).then_inc(qk_loaded, 16)

                def load_v(n, u):
                    sp.dma_start(vq[u][:].rearrange("p j h w -> p j (h w)"),
                                 v_scr.rearrange("b g p j w -> (b g) p j w")[n]).then_inc(v_loaded, 16)

                def put_maxima(done, u):
                    sp_alone.wait_ge(ring_done, done)
                    for s in range(PARTS):
                        sp.dma_start(qs[u][KROWS + s:KROWS + s + 1, :, :], mparts[:, s, :]).then_inc(m_landed, 16)

                def store_z(n, c, done):
                    sp_alone.wait_ge(ring_done, done)
                    sp.dma_start(zn_scr[n, c], zn[c % 2][:].rearrange("p t h d -> p t (h d)")).then_inc(zn_stored[c % 2], 16)

                def group(n, u, has_prev, has_next):
                    if has_next:
                        if has_prev:
                            sp.wait_ge(sc_ready, 2 * NS * n)
                        load_qk(n + 1, 1 - u)
                        if has_prev:
                            sp.wait_ge(pv_done, NS * n)
                        load_v(n + 1, 1 - u)
                    done = ring_base(n)
                    for jobs in ring_jobs(has_prev, has_next):
                        for job in jobs:
                            done = done + 1
                            if job[0] == "z":
                                store_z(n - 1 if job[2] else n, job[1], done)
                            if job[0] == "turn":
                                put_maxima(done, 1 - u)
                    if not has_next:
                        store_z(n, CB - 1, done + 1)

                load_qk(0, 0)
                load_v(0, 0)
                put_maxima(NM + 1, 0)
                groups(sp, group)
                for u in range(2):
                    sp.wait_ge(zn_stored[u], 16 * CB * QUADS // 2)

            @block.gpsimd
            def _(pool):
                pool_alone = Alone(pool, pool_tick)
                def group(n, u, has_prev, has_next):
                    for s, (c, j) in enumerate(STEPS):
                        q0 = CH - width(c, j)
                        if j < TT * c:
                            continue
                        for p in range(2):
                            pool_alone.wait_ge(exp_done, 2 * NS * n + 2 * s + p + 1)
                            tile = pr[p][s % 2][:, :, q0:q0 + P]
                            nc.gpsimd.affine_select(out=tile, in_=tile, compare_op=ALU.is_ge, fill=0.0, base=0,
                                                    pattern=[[0, 2], [1, P]], channel_multiplier=-1).then_inc(masked, 1)

                groups(pool, group)

            @block.scalar
            def _(act):
                def z_out(n, c, has_next):
                    g = CB * n + c
                    act.wait_ge(pv_done, NS * n + FIRST[c + 1])
                    if late(g, 2):
                        act.wait_ge(ring_done, uses_to_z(n, c - 2, has_next) if c >= 2 else uses_to_z(n - 1, c + CB - 2, True))
                    nc.scalar.activation(zt[c % 2][:], pv[:], ACT.Copy).then_inc(zt_done, 1)

                def group(n, u, has_prev, has_next):
                    for s, (c, j) in enumerate(STEPS):
                        q0 = CH - width(c, j)
                        for p in range(2):
                            act.wait_ge(sc_ready, 2 * NS * n + 2 * s + p + 1)
                            if has_prev or s >= 2:
                                act.wait_ge(pv_done, NS * n + s - 1)
                            nc.scalar.activation(pr[p][s % 2][:, :, q0:], sc[p][:, :, q0:], ACT.Exp).then_inc(exp_done, 1)
                        if j == 0 and c > 0:
                            z_out(n, c - 1, has_next)
                        if s == 0 and has_prev:
                            z_out(n - 1, CB - 1, True)

                groups(act, group)
                z_out(QUADS - 1, CB - 1, False)

            @block.tensor
            def _(pe):
                def ring_slot(base, k):
                    if k >= RING:
                        pe.wait_ge(ring_done, base + k - RING + 1)
                    elif not (isinstance(base, int) and base == 0):
                        pe.wait_ge(ring_done, base)
                    return ring[k % RING]

                def ring_job(job, base, k, n, u, queue_u):
                    bank = ring_slot(base, k)
                    if job[0] == "max":
                        h, t, kc = MAXIMA[job[1]]
                        w = CH if kc < t // TT else (t % TT + 1) * P
                        pe.matmul(bank[:, 0:w], qs[queue_u][0:KROWS, h, t * P:(t + 1) * P], ks[queue_u][0:KROWS, h, kc * CH:kc * CH + w],
                                  start=True, stop=True).then_inc(ring_ready, 1)
                    if job[0] == "turn":
                        pe.wait_ge(negm_ready, n + 2)
                        pe.transpose(bank[:, 0:P], negm[:], ident[:]).then_inc(ring_ready, 1)
                    if job[0] == "z":
                        c = job[1]
                        pe.wait_ge(zt_done, CB * (n - 1 if job[2] else n) + c + 1)
                        for t in range(TT):
                            ins = pe.transpose(bank[:, t * P:(t + 1) * P], zt[c % 2][:, t * P:(t + 1) * P], ident[:])
                        ins.then_inc(ring_ready, 1)

                def scores(n, u, s, p):
                    c, j = STEPS[s]
                    q0 = CH - width(c, j)
                    if s > 0 or not (isinstance(n, int) and n == 0):
                        pe.wait_ge(exp_done, 2 * NS * n + 2 * s + p - 1)
                    for a in range(2):
                        h = 2 * p + a
                        ins = pe.matmul(sc[p][:, a, q0:], ks[u][:, h, j * P:(j + 1) * P], qs[u][:, h, c * CH + q0:(c + 1) * CH],
                                        start=True, stop=True)
                    ins.then_inc(sc_ready, 1)

                def values(n, u, s):
                    c, j = STEPS[s]
                    q0 = CH - width(c, j)
                    if j == 0:
                        pe.wait_ge(v_loaded, 16 * (n + 1))
                        if c > 0 or not (isinstance(n, int) and n == 0):
                            pe.wait_ge(zt_done, CB * n + c)
                    if j >= TT * c:
                        pe.wait_ge(masked, DIAG * n + 2 * j + 2)
                    else:
                        pe.wait_ge(exp_done, 2 * NS * n + 2 * s + 2)
                    for h in range(GH):
                        ins = pe.matmul(pv[VW * h:VW * (h + 1), q0:], vq[u][:, j, h], pr[h // 2][s % 2][:, h % 2, q0:],
                                        start=j == 0, stop=j == TT * (c + 1) - 1)
                    ins.then_inc(pv_done, 1)

                def group(n, u, has_prev, has_next):
                    base, k = ring_base(n), 0
                    pe.wait_ge(m_landed, 16 * PARTS * (n + 1))
                    for s, jobs in enumerate(ring_jobs(has_prev, has_next)):
                        if s == M_FROM and has_next:
                            pe.wait_ge(qk_loaded, QKD * (n + 2))
                        half = (len(jobs) + 1) // 2
                        scores(n, u, s, 0)
                        for job in jobs[:half]:
                            ring_job(job, base, k, n, u, 1 - u)
                            k += 1
                        scores(n, u, s, 1)
                        if s > 0:
                            values(n, u, s - 1)
                        elif has_prev:
                            values(n - 1, 1 - u, NS - 1)
                        for job in jobs[half:]:
                            ring_job(job, base, k, n, u, 1 - u)
                            k += 1
                    return k

                pe.wait_ge(qk_loaded, QKD)
                pe.wait_ge(set_up, 4)
                for k in range(NM):
                    ring_job(("max", k), 0, k, -1, 0, 0)
                ring_job(("turn",), 0, NM, -1, 0, 0)
                groups(pe, group)
                values(QUADS - 1, 1, NS - 1)
                ring_job(("z", CB - 1, False), ring_base(QUADS - 1), CB, QUADS - 1, 1, 1)

            @block.vector
            def _(dve):
                dve_alone = Alone(dve, dve_tick)
                def ring_job(job, done, n, bank, m_before):
                    if job[0] != "max":
                        dve.wait_ge(ring_done, done)
                    if job[0] == "turn":
                        nc.vector.tensor_reduce(negm[:, 0:GH * KT], mx[:].rearrange("p h t k -> p (h t) k"), AX.X, ALU.max,
                                                negate=True).then_inc(negm_ready, 1)
                    dve_alone.wait_ge(ring_ready, done + 1)
                    if job[0] == "max":
                        h, t, kc = MAXIMA[job[1]]
                        to = mx[:, h, t, kc:kc + 1]
                        if job[1] == 0:
                            if m_before:
                                dve_alone.wait_ge(negm_ready, n + 1)
                        if kc < t // TT:
                            nc.vector.tensor_reduce(to, bank[:], AX.X, ALU.max).then_inc(ring_done, 1)
                        else:
                            w = (t % TT + 1) * P
                            nc.vector.tensor_tensor_reduce(out=bank[:, 0:w], in0=bank[:, 0:w], in1=mask[:, CH - w:CH], scale=1.0,
                                                           scalar=NEG, op0=ALU.add, op1=ALU.max, accum_out=to).then_inc(ring_done, 1)
                    if job[0] == "turn":
                        if m_before:
                            dve.wait_ge(m_landed, 16 * PARTS * (n + 1))
                        rows = bank[0:GH * KT, 0:P]
                        base = 3 * (n + 1)
                        nc.vector.tensor_copy(mparts[:, 0], rows).then_inc(m_step, 1)
                        dve.wait_ge(m_step, base + 1)
                        nc.vector.tensor_tensor(mrest[:], rows, mparts[:, 0], ALU.subtract).then_inc(m_step, 1)
                        dve.wait_ge(m_step, base + 2)
                        nc.vector.tensor_copy(mparts[:, 1], mrest[:]).then_inc(m_step, 1)
                        dve.wait_ge(m_step, base + 3)
                        nc.vector.tensor_tensor(mparts[:, 2], mrest[:], mparts[:, 1], ALU.subtract).then_inc(ring_done, 1)
                    if job[0] == "z":
                        nn, c = (n - 1 if job[2] else n), job[1]
                        g = CB * nn + c
                        z = bank[:].rearrange("p (t h w) -> p t h w", t=TT, h=GH)
                        nc.vector.reciprocal(rl[:], z[:, :, :, DH]).then_inc(rl_ready, 1)
                        dve.wait_ge(rl_ready, g + 1)
                        if late(g, 2):
                            dve.wait_ge(zn_stored[c % 2], 16 * turns(nn, c))
                        nc.vector.tensor_tensor(zn[c % 2][:], z[:, :, :, 0:DH], rl[:].unsqueeze(3).broadcast_to([P, TT, GH, DH]),
                                                ALU.mult).then_inc(ring_done, 1)

                def group(n, u, has_prev, has_next):
                    base, k = ring_base(n), 0
                    for jobs in ring_jobs(has_prev, has_next):
                        for job in jobs:
                            ring_job(job, base + k, n, ring[k % RING], True)
                            k += 1

                for u in range(2):
                    nc.vector.memset(ks[u][KROWS:KMAX], 1.0).then_inc(set_up, 1)
                nc.vector.memset(mx[:], NEG).then_inc(set_up, 1)
                nc.vector.memset(negm[:], 0.0).then_inc(set_up, 1)

                dve.wait_ge(set_up, 4)
                for k in range(NM):
                    ring_job(("max", k), k, -1, ring[k % RING], False)
                ring_job(("turn",), NM, -1, ring[NM % RING], False)
                groups(dve, group)
                ring_job(("z", CB - 1, False), ring_base(QUADS - 1) + CB, QUADS - 1, ring[CB % RING], True)


HT = HID // P
HB = 4
ZR = DH + 2


def feed(nc, const, x, W1T, b1, W2T, b2, WO, bO, scale, xnT_scr, lt_scr, zn_scr, out):
    ident = const["ident"]
    with ExitStack() as ctx:
        sb = lambda name, shape, dt=F32: ctx.enter_context(nc.sbuf_tensor(name, shape, dt))
        sem = lambda name: ctx.enter_context(nc.semaphore(name))
        w1t = sb("w1t", [P, KD, HID])
        w2t = sb("w2t", [P, HT, D])
        next1 = sb("next1", [P, KD, HID])
        next2 = sb("next2", [P, HT, D])
        eff1 = sb("eff1", [P, KD, HID])
        eff2 = sb("eff2", [P, HT, D])
        b1c = sb("b1c", [P, HT])
        wo = sb("wo", [ZR, D])
        scale_c = sb("scale_c", [P, 1])
        even = sb("even", [P, 2 * RANKS, D])
        first = sb("first", [P, KD, LORA + 4])
        odd = sb("odd", [P, KD, 2 * RANKS])
        xc = [sb(f"xc{u}", [P, KD, CH]) for u in range(2)]
        x_res = [sb(f"x_res{u}", [P, TT, D]) for u in range(2)]
        zn_in = [sb(f"zn_in{u}", [P, QB, TT, GH * DH]) for u in range(2)]
        zs = [sb(f"zs{u}", [P, TT, ZR]) for u in range(2)]
        zT = [sb(f"zT{u}", [ZR, CH]) for u in range(2)]
        g = [sb(f"g{u}", [P, HT, CH]) for u in range(2)]
        y = [sb(f"y{u}", [P, TT, D]) for u in range(2)]
        ps_h = [ctx.enter_context(nc.psum_tensor(f"ps_h{k}", [P, CH], F32)) for k in range(HB)]
        ps_y = [ctx.enter_context(nc.psum_tensor(f"ps_y{k}", [P, CH], F32)) for k in range(2)]
        ps_z = ctx.enter_context(nc.psum_tensor("ps_z", [P, CH], F32))

        w_loaded = sem("feed_w_loaded")
        scale_loaded = sem("feed_scale")
        ones_set = sem("feed_ones_set")
        first_loaded = sem("feed_first")
        odd_ready = sem("feed_odd_ready")
        outer = sem("feed_outer")
        next_ready = sem("feed_next_ready")
        eff1_ready = sem("feed_eff1_ready")
        eff2_ready = sem("feed_eff2_ready")
        xc_loaded = [sem(f"feed_xc_loaded{u}") for u in range(2)]
        x_loaded = [sem(f"feed_x_loaded{u}") for u in range(2)]
        z_loaded = [sem(f"feed_z_loaded{u}") for u in range(2)]
        zs_ready = sem("feed_zs_ready")
        z_turned = sem("feed_z_turned")
        zT_ready = sem("feed_zT_ready")
        h_ready = sem("feed_h_ready")
        g_ready = sem("feed_g_ready")
        y_made = sem("feed_y_made")
        y_ready = sem("feed_y_ready")
        y_stored = [sem(f"feed_y_stored{u}") for u in range(2)]
        W_DMAS = 6

        pool_tick = sem("pool_tick3")

        with nc.Block() as block:
            @block.sync
            def _(sp):
                sp.dma_start(w1t[:], W1T.rearrange("(c p) h -> p c h", p=P)).then_inc(w_loaded, 16)
                sp.dma_start(w2t[:], W2T.rearrange("(c p) o -> p c o", p=P)).then_inc(w_loaded, 16)
                sp.dma_start(b1c[:], b1.rearrange("(c p) -> p c", p=P), allow_slow_non_contiguous=True).then_inc(w_loaded, 16)
                sp.dma_start(wo[0:DH], WO).then_inc(w_loaded, 16)
                sp.dma_start(wo[DH:DH + 1], bO.rearrange("(a n) -> a n", a=1)).then_inc(w_loaded, 16)
                sp.dma_start(wo[DH + 1:DH + 2], b2.rearrange("(a n) -> a n", a=1)).then_inc(w_loaded, 16)

                def load(b, c):
                    m, u = b * CB + c, c % 2
                    if late(m, 2):
                        sp.wait_ge(h_ready, HT * (m - 1))
                    sp.dma_start(xc[u][:], xnT_scr[m]).then_inc(xc_loaded[u], 16)
                    if late(m, 2):
                        sp.wait_ge(zs_ready, m - 1)
                    sp.dma_start(zn_in[u][:].rearrange("p q t w -> p q (t w)"),
                                 zn_scr.rearrange("(b q) c p t w -> b c p q (t w)", q=QB)[b, c]).then_inc(z_loaded[u], 16)
                    if late(m, 2):
                        sp.wait_ge(y_ready, TT * (m - 1))
                    sp.dma_start(x_res[u][:], x[b, c * CH:(c + 1) * CH, :].rearrange("(t p) d -> p t d", p=P)).then_inc(x_loaded[u], 16)

                def store(b, c):
                    m, u = b * CB + c, c % 2
                    sp.wait_ge(y_ready, TT * (m + 1))
                    sp.dma_start(out[b, c * CH:(c + 1) * CH, :].rearrange("(t p) d -> p t d", p=P), y[u][:]).then_inc(y_stored[u], 16)

                pipelined(sp, load, store, lag=2)
                for u in range(2):
                    sp.wait_ge(y_stored[u], 16 * NCH // 2)

            @block.gpsimd
            def _(pool):
                pool_alone = Alone(pool, pool_tick)
                pool.dma_start(scale_c[:], scale.broadcast_to([P, 1])).then_inc(scale_loaded, 16)
                for u in range(2):
                    nc.gpsimd.memset(zs[u][:, :, DH:DH + 1], float(H)).then_inc(ones_set, 1)
                    nc.gpsimd.memset(zs[u][:, :, DH + 1:DH + 2], 1.0).then_inc(ones_set, 1)
                pool.wait_ge(scale_loaded, 16)
                pool.wait_ge(w_loaded, 16 * W_DMAS)

                def prepare(b):
                    if late(b, 1):
                        pool_alone.wait_ge(outer, 2 * b)
                    pool.dma_start(even[:], lt_scr[b * CB].rearrange("(i two) d -> two i d", two=2)[0:1].broadcast_to([P, 2 * RANKS, D])
                                   ).then_inc(first_loaded, 16)
                    pool.dma_start(first[:], xnT_scr[b * CB][:, :, 0:LORA + 4]).then_inc(first_loaded, 16)
                    pool_alone.wait_ge(first_loaded, 32 * (b + 1))
                    nc.gpsimd.tensor_scalar(odd[:], first[:, :, 2:2 + LORA:2], scale_c[:, 0:1], None, ALU.mult).then_inc(odd_ready, 1)
                    pool_alone.wait_ge(odd_ready, b + 1)
                    if late(b, 1):
                        pool_alone.wait_ge(eff1_ready, b)
                    for c in range(KD):
                        for i in range(RANKS):
                            ins = nc.gpsimd.tensor_scalar(next1[:, c, D * i:D * (i + 1)], even[:, i], odd[:, c, i:i + 1], 1.0, ALU.mult, ALU.mult)
                    ins.then_inc(outer, 1)
                    if late(b, 1):
                        pool_alone.wait_ge(eff2_ready, b)
                    for k in range(HT):
                        for i in range(RANKS):
                            w = D // RANKS
                            ins = nc.gpsimd.tensor_scalar(next2[:, k, w * i:w * (i + 1)], even[:, RANKS + i, k // KD::RANKS],
                                                          odd[:, k % KD, RANKS + i:RANKS + i + 1], 1.0, ALU.mult, ALU.mult)
                    ins.then_inc(outer, 1)
                    pool_alone.wait_ge(outer, 2 * b + 2)
                    nc.gpsimd.tensor_tensor(next1[:], next1[:], w1t[:], ALU.add).then_inc(next_ready, 1)
                    nc.gpsimd.tensor_tensor(next2[:], next2[:], w2t[:], ALU.add).then_inc(next_ready, 1)

                prepare(0)
                with pool.Fori(1, B) as b:
                    prepare(b)

            @block.scalar
            def _(act):
                act.wait_ge(w_loaded, 16 * W_DMAS)

                def gelu(b, c):
                    m, u = b * CB + c, c % 2
                    act.wait_ge(z_turned, m + 1)
                    if late(m, 2):
                        act.wait_ge(y_made, TT * (m - 1))
                    nc.scalar.activation(zT[u][:], ps_z[0:ZR], ACT.Identity).then_inc(zT_ready, 1)
                    for k in range(HT):
                        act.wait_ge(h_ready, HT * m + k + 1)
                        nc.scalar.activation(g[u][:, k], ps_h[k % HB][:], ACT.Gelu, bias=b1c[:, k:k + 1]).then_inc(g_ready, 1)

                pipelined(act, gelu, lambda b, c: None)

            @block.tensor
            def _(pe):
                pe.wait_ge(w_loaded, 16 * W_DMAS)

                def hidden(b, c):
                    m, u = b * CB + c, c % 2
                    pe.wait_ge(zs_ready, m + 1)
                    if late(m, 1):
                        pe.wait_ge(zT_ready, m)
                    for t in range(TT):
                        ins = pe.transpose(ps_z[0:ZR, t * P:(t + 1) * P], zs[u][:, t], ident[:])
                    ins.then_inc(z_turned, 1)
                    pe.wait_ge(xc_loaded[u], 16 * (turns(b, c) + 1))
                    if c == 0:
                        pe.wait_ge(eff1_ready, b + 1)
                    for k in range(HT):
                        if late(m, 1) or k >= HB:
                            pe.wait_ge(g_ready, HT * m + k - HB + 1)
                        for d in range(KD):
                            ins = pe.matmul(ps_h[k % HB][:], eff1[:, d, k * P:(k + 1) * P], xc[u][:, d], start=d == 0, stop=d == KD - 1)
                        ins.then_inc(h_ready, 1)

                def outputs(b, c):
                    m, u = b * CB + c, c % 2
                    pe.wait_ge(g_ready, HT * (m + 1))
                    pe.wait_ge(zT_ready, m + 1)
                    if c == 0:
                        pe.wait_ge(eff2_ready, b + 1)
                    for t in range(TT):
                        if late(m, 1) or t >= 2:
                            pe.wait_ge(y_ready, TT * m + t - 1)
                        to = ps_y[t % 2][:, 0:D]
                        pe.matmul(to, zT[u][:, t * P:(t + 1) * P], wo[:], start=True, stop=False)
                        for k in range(HT):
                            ins = pe.matmul(to, g[u][:, k, t * P:(t + 1) * P], eff2[:, k], start=False, stop=k == HT - 1)
                        ins.then_inc(y_made, 1)

                pipelined(pe, hidden, outputs)

            @block.vector
            def _(dve):
                dve.wait_ge(ones_set, 4)

                def gather(b, c):
                    m, u = b * CB + c, c % 2
                    dve.wait_ge(z_loaded[u], 16 * (turns(b, c) + 1))
                    if late(m, 2):
                        dve.wait_ge(z_turned, m - 1)
                    for t in range(TT):
                        ins = nc.vector.tensor_reduce(zs[u][:, t, 0:DH], zn_in[u][:, :, t].rearrange("p q (h d) -> p d q h", d=DH), AX.XY, ALU.add)
                    ins.then_inc(zs_ready, 1)
                    if c == 0:
                        dve.wait_ge(next_ready, 2 * b + 2)
                        if late(b, 1):
                            dve.wait_ge(h_ready, HT * m)
                        nc.vector.tensor_copy(eff1[:], next1[:]).then_inc(eff1_ready, 1)
                    if c == 1:
                        if late(b, 1):
                            dve.wait_ge(y_made, TT * (m - 1))
                        nc.vector.tensor_copy(eff2[:], next2[:]).then_inc(eff2_ready, 1)

                def finish(b, c):
                    m, u = b * CB + c, c % 2
                    dve.wait_ge(x_loaded[u], 16 * (turns(b, c) + 1))
                    if late(m, 2):
                        dve.wait_ge(y_stored[u], 16 * turns(b, c))
                    for t in range(TT):
                        dve.wait_ge(y_made, TT * m + t + 1)
                        nc.vector.tensor_tensor(y[u][:, t], ps_y[t % 2][:, 0:D], x_res[u][:, t], ALU.add).then_inc(y_ready, 1)

                pipelined(dve, gather, finish)


def program(nc, x, WQ, bQ, WK, bK, WV, bV, WO, bO, W1T, b1, W2T, b2, scale, out):
    scr = lambda name, shape, dt=F32: nc.dram_tensor(name, shape, dt, kind="Internal").ap()
    qk_scr = scr("qk_scr", [2, PARTS, B, D, S], BF16)
    v_scr = scr("v_scr", [B, QB, P, KT, GH * VW])
    xnT_scr = scr("xnT_scr", [NCH, P, KD, CH])
    lt_scr = scr("lt_scr", [NCH, LORA, D])
    zn_scr = scr("zn_scr", [QUADS, CB, P, TT, GH * DH])
    with ExitStack() as ctx:
        const = {
            "ident": ctx.enter_context(nc.sbuf_tensor("ident", [P, P], F32)),
            "mask": ctx.enter_context(nc.sbuf_tensor("mask", [P, CH], F32)),
        }
        project(nc, const, x, WQ, bQ, WK, bK, WV, bV, qk_scr, v_scr, xnT_scr, lt_scr)
        attend(nc, const, qk_scr, v_scr, zn_scr)
        feed(nc, const, x, W1T, b1, W2T, b2, WO, bO, scale, xnT_scr, lt_scr, zn_scr, out)


def kernel(**inputs):
    import numpy as np
    import concourse.bacc as bacc
    from concourse.bass_utils import run_bass_kernel_spmd

    a = {k.removeprefix("L0_attn_").removeprefix("L0_ffn_"): np.asarray(v) for k, v in inputs.items()}
    arrays = {
        "x": a["x"], "WQ": a["WQ"], "bQ": a["bQ"], "WK": a["WK"], "bK": a["bK"], "WV": a["WV"], "bV": a["bV"],
        "WO": a["WO"], "bO": a["bO"], "W1T": a["W1"].T, "b1": a["b1"], "W2T": a["W2"].T, "b2": a["b2"],
        "scale": a["scale"].reshape(1, 1),
    }
    nc = bacc.Bacc("TRN2", target_bir_lowering=False, num_devices=1)
    given, aps = {}, []
    for name, v in arrays.items():
        v = np.ascontiguousarray(v)
        given[f"in_{name}"] = v
        aps.append(nc.dram_tensor(f"in_{name}", v.shape, mybir.dt.from_np(v.dtype), kind="ExternalInput").ap())
    out = nc.dram_tensor("out_y", (B, S, D), F32, kind="ExternalOutput").ap()
    program(nc, *aps, out)
    r = run_bass_kernel_spmd(nc, [given], core_ids=[0])
    return r.results[0]["out_y"]
```

```python
from contextlib import ExitStack

import concourse.bass as bass
from concourse import mybir
from concourse.alu_op_type import AluOpType as ALU

ACT = mybir.ActivationFunctionType
AX = mybir.AxisListType
F32 = mybir.dt.float32
BF16 = mybir.dt.bfloat16

P = 128
B, S, D, H = 4, 2048, 256, 16
DH = D // H
HID = 1024
TOK = B * S
KD = D // P
CH = 512
CB = S // CH
NCH = TOK // CH
TT = CH // P
GH = 4
QUADS = B * H // GH
QB = H // GH
KT = S // P
VW = 32
PARTS = 3
TERMS = [(0, 0), (0, 1), (1, 0), (1, 1), (0, 2), (2, 0)]
KROWS = len(TERMS) * DH
KMAX = KROWS + PARTS
EPS = 1e-5
NEG = -1e30
LORA = 16
RANKS = 4


def late(m, k):
    return not isinstance(m, int) or m >= k


def turns(b, c):
    return b * (CB // 2) + c // 2


class Alone:

    def __init__(self, eng, tick):
        self.eng, self.tick = eng, tick

    def wait_ge(self, sem, value):
        self.eng.wait_ge(sem, value)
        if not isinstance(value, int):
            self.eng.sem_inc(self.tick, 1)


def pipelined(eng, *stages):
    def steps(b):
        for c in range(CB):
            for stage, lag in stages:
                if b is None:
                    if c >= lag:
                        stage(0, c - lag)
                else:
                    stage(b if c >= lag else b - 1, (c - lag) % CB)

    steps(None)
    with eng.Fori(1, B) as b:
        steps(b)
    for k in range(1, CB):
        for stage, lag in stages:
            if k <= lag:
                stage(B - 1, CB - 1 - lag + k)


def project(nc, const, x, WQ, bQ, WK, bK, WV, bV, qk_scr, v_scr, xnT_scr, lt_scr):
    ident = const["ident"]
    with ExitStack() as ctx:
        sb = lambda name, shape, dt=F32: ctx.enter_context(nc.sbuf_tensor(name, shape, dt))
        sem = lambda name: ctx.enter_context(nc.semaphore(name))
        w_sb = sb("w_sb", [P, 3, KD, D])
        b_in = sb("b_in", [P, 2, 2])
        b_sb = sb("b_sb", [P, 2, 2])
        bv_sb = sb("bv_sb", [P, D])
        x_in = sb("x_in", [P, 2, TT, D])
        xn = sb("xn", [P, 2, TT, D])
        xnT = sb("xnT", [P, 2, KD, CH])
        stats = sb("stats", [P, 2, TT, 6])
        mv = sb("mv", [P, 2, TT, 2])
        veps = sb("veps", [P, 2, TT])
        nmean = sb("nmean", [P, 2, TT])
        std = sb("std", [P, 2, TT])
        rstd = sb("rstd", [P, 2, TT])
        qk32 = sb("qk32", [P, 2, 4, CH])
        parts = sb("parts", [P, 2, 4, PARTS, CH], BF16)
        rest = sb("rest", [P, 4, CH])
        vp = sb("vp", [P, 2, TT, H, VW])
        psT = [ctx.enter_context(nc.psum_tensor(f"psT{d}", [P, CH], F32)) for d in range(KD)]
        psQK = [ctx.enter_context(nc.psum_tensor(f"psQK{k}", [P, CH], F32)) for k in range(4)]
        psV = [ctx.enter_context(nc.psum_tensor(f"psV{k}", [P, 2, D], F32)) for k in range(2)]

        w_loaded = sem("w_loaded")
        x_loaded = [sem(f"x_loaded{u}") for u in range(2)]
        const_ready = sem("const_ready")
        bias_ready = sem("bias_ready")
        stat_step = sem("stat_step")
        var_ready = sem("var_ready")
        std_ready = sem("std_ready")
        rstd_ready = sem("rstd_ready")
        xn_ready = sem("xn_ready")
        xT_ready = sem("xT_ready")
        xnT_ready = sem("xnT_ready")
        qk_ready = sem("qk_ready")
        qk_out = sem("qk_out")
        hi_ready = sem("hi_ready")
        rest_ready = sem("rest_ready")
        low_ready = sem("low_ready")
        v_ready = sem("v_ready")
        v_out = sem("v_out")
        mid_ready = sem("mid_ready")
        lt_stored, xnT_stored, qk_stored, v_stored = ([sem(f"{name}_stored{u}") for u in range(2)]
                                                      for name in ("lt", "xnT", "qk", "v"))

        W_DMAS = 3 + 2 + 1

        pool_tick, dve_tick, sp_tick = sem("pool_tick1"), sem("dve_tick1"), sem("sp_tick1")

        with nc.Block() as block:
            @block.sync
            def _(sp):
                sp_alone = Alone(sp, sp_tick)
                for k, w in enumerate((WQ, WK, WV)):
                    sp.dma_start(w_sb[:, k], w.rearrange("(c p) n -> p c n", p=P)).then_inc(w_loaded, 16)
                for k, b in enumerate((bQ, bK)):
                    sp.dma_start(b_in[:, k], b.rearrange("(g p) -> p g", p=P), allow_slow_non_contiguous=True).then_inc(w_loaded, 16)
                sp.dma_start(bv_sb[:, :], bV.rearrange("(a n) -> a n", a=1).broadcast_to([P, D])).then_inc(w_loaded, 16)

                def load(b, c):
                    m = b * CB + c
                    if late(m, 2):
                        sp.wait_ge(xn_ready, m - 1)
                    sp.dma_start(x_in[:, c % 2], x[b, c * CH:(c + 1) * CH, :].rearrange("(t p) d -> p t d", p=P)).then_inc(x_loaded[c % 2], 16)

                def store_norm(b, c):
                    m, u = b * CB + c, c % 2
                    sp.wait_ge(xn_ready, m + 1)
                    sp.dma_start(lt_scr[m], xn[1:1 + LORA, u, 0, :]).then_inc(lt_stored[u], 16)
                    sp.wait_ge(xnT_ready, m + 1)
                    sp.dma_start(xnT_scr[m], xnT[:, u]).then_inc(xnT_stored[u], 16)

                def store_qkv(b, c):
                    m, u = b * CB + c, c % 2
                    sp_alone.wait_ge(low_ready, 4 * (m + 1))
                    for k in range(4):
                        sp.dma_start(qk_scr[k // 2, :, b, P * (k % 2):P * (k % 2 + 1), c * CH:(c + 1) * CH].rearrange("s r t -> r s t"),
                                     parts[:, u, k]).then_inc(qk_stored[u], 16)
                    sp.wait_ge(v_out, 2 * m + 2)
                    for g in range(QB):
                        sp.dma_start(v_scr[b, g, :, c * TT:(c + 1) * TT, :],
                                     vp[:, u, :, GH * g:GH * (g + 1)].rearrange("p t h w -> p t (h w)")).then_inc(v_stored[u], 16)

                pipelined(sp, (load, 0), (store_norm, 2), (store_qkv, 3))
                for u in range(2):
                    sp.wait_ge(lt_stored[u], 16 * NCH // 2)
                    sp.wait_ge(xnT_stored[u], 16 * NCH // 2)
                    sp.wait_ge(qk_stored[u], 16 * 4 * NCH // 2)
                    sp.wait_ge(v_stored[u], 16 * QB * NCH // 2)

            @block.gpsimd
            def _(pool):
                pool_alone = Alone(pool, pool_tick)
                nc.gpsimd.memset(ident[:], 0.0).then_inc(const_ready, 1)
                nc.gpsimd.memset(const["mask"][:], 0.0).then_inc(const_ready, 1)
                nc.gpsimd.memset(vp[:], 0.0).then_inc(const_ready, 1)
                pool.wait_ge(const_ready, 3)
                nc.gpsimd.affine_select(out=ident[:], in_=ident[:], compare_op=ALU.not_equal, fill=1.0, base=0,
                                        pattern=[[-1, P]], channel_multiplier=1).then_inc(const_ready, 1)
                nc.gpsimd.affine_select(out=const["mask"][:, 2 * CH - P:], in_=const["mask"][:, 2 * CH - P:], compare_op=ALU.is_ge,
                                        fill=NEG, base=0, pattern=[[-1, P]], channel_multiplier=1).then_inc(const_ready, 1)
                nc.gpsimd.memset(vp[:, :, :, :, DH:DH + 1], 1.0).then_inc(const_ready, 1)

                def norm(b, c):
                    m, u = b * CB + c, c % 2
                    pool_alone.wait_ge(rstd_ready, m + 1)
                    if late(m, 2):
                        pool_alone.wait_ge(xT_ready, m - 1)
                        pool_alone.wait_ge(lt_stored[u], 16 * turns(b, c))
                    for t in range(TT):
                        ins = nc.gpsimd.tensor_scalar(xn[:, u, t], x_in[:, u, t], nmean[:, u, t:t + 1], rstd[:, u, t:t + 1],
                                                      ALU.add, ALU.mult)
                    ins.then_inc(xn_ready, 1)

                def high(b, c):
                    m, u = b * CB + c, c % 2
                    if late(m, 2):
                        pool_alone.wait_ge(qk_stored[u], 16 * 4 * turns(b, c))
                    for k in range(4):
                        pool_alone.wait_ge(qk_out, 4 * m + k + 1)
                        nc.gpsimd.tensor_scalar(parts[:, u, k, 0], qk32[:, u, k], 1.0, 0.0, ALU.mult, ALU.add).then_inc(hi_ready, 1)

                pipelined(pool, (norm, 0), (high, 2))

            @block.scalar
            def _(act):
                act.wait_ge(w_loaded, 16 * W_DMAS)
                nc.scalar.activation(b_sb[:, 0], b_in[:, 0], ACT.Identity, scale=0.25).then_inc(bias_ready, 1)
                nc.scalar.activation(b_sb[:, 1], b_in[:, 1], ACT.Identity).then_inc(bias_ready, 1)
                act.wait_ge(bias_ready, 2)

                def root(b, c):
                    m, u = b * CB + c, c % 2
                    act.wait_ge(var_ready, m + 1)
                    nc.scalar.activation(std[:, u], veps[:, u], ACT.Sqrt).then_inc(std_ready, 1)

                def turn(b, c):
                    m, u = b * CB + c, c % 2
                    act.wait_ge(xT_ready, m + 1)
                    if late(m, 2):
                        act.wait_ge(v_ready, 2 * (m - 1))
                        act.wait_ge(xnT_stored[u], 16 * turns(b, c))
                    for d in range(KD):
                        ins = nc.scalar.activation(xnT[:, u, d], psT[d][:], ACT.Identity)
                    ins.then_inc(xnT_ready, 1)

                def out(b, c):
                    m, u = b * CB + c, c % 2
                    if late(m, 2):
                        act.wait_ge(rest_ready, 4 * (m - 1))
                    for k in range(5):
                        if k < 4:
                            act.wait_ge(qk_ready, 4 * m + k + 1)
                            nc.scalar.activation(qk32[:, u, k], psQK[k][:], ACT.Identity, bias=b_sb[:, k // 2, k % 2:k % 2 + 1],
                                                 scale=0.25 if k < 2 else 1.0).then_inc(qk_out, 1)
                        if k > 0:
                            act.wait_ge(rest_ready, 4 * m + k)
                            nc.scalar.activation(parts[:, u, k - 1, 1], rest[:, k - 1], ACT.Copy).then_inc(mid_ready, 1)

                pipelined(act, (root, 0), (turn, 1), (out, 2))

            @block.tensor
            def _(pe):
                pe.wait_ge(const_ready, 6)
                pe.wait_ge(w_loaded, 16 * W_DMAS)

                def turn(b, c):
                    m, u = b * CB + c, c % 2
                    pe.wait_ge(xn_ready, m + 1)
                    if late(m, 1):
                        pe.wait_ge(xnT_ready, m)
                    for t in range(TT):
                        for d in range(KD):
                            ins = pe.transpose(psT[d][:, t * P:(t + 1) * P], xn[:, u, t, d * P:(d + 1) * P], ident[:])
                    ins.then_inc(xT_ready, 1)

                def products(b, c):
                    m, u = b * CB + c, c % 2
                    pe.wait_ge(xnT_ready, m + 1)
                    for k in range(4):
                        if late(m, 1):
                            pe.wait_ge(qk_out, 4 * m - 3 + k)
                        for d in range(KD):
                            ins = pe.matmul(psQK[k][:], w_sb[:, k // 2, d, (k % 2) * P:(k % 2 + 1) * P], xnT[:, u, d],
                                            start=d == 0, stop=d == KD - 1)
                        ins.then_inc(qk_ready, 1)
                    for t in range(TT):
                        if t % 2 == 0 and late(m, 1):
                            pe.wait_ge(v_out, 2 * m - 1 + t // 2)
                        for d in range(KD):
                            ins = pe.matmul(psV[t // 2][:, t % 2], xnT[:, u, d, t * P:(t + 1) * P], w_sb[:, 2, d],
                                            start=d == 0, stop=d == KD - 1)
                        if t % 2 == 1:
                            ins.then_inc(v_ready, 1)

                pipelined(pe, (turn, 1), (products, 2))

            @block.vector
            def _(dve):
                dve_alone = Alone(dve, dve_tick)
                dve.wait_ge(w_loaded, 16 * W_DMAS)
                dve.wait_ge(const_ready, 6)

                def statistics(b, c):
                    m, u = b * CB + c, c % 2
                    dve.wait_ge(x_loaded[u], 16 * (turns(b, c) + 1))
                    for t in range(TT):
                        ins = nc.vector.bn_stats(stats[:, u, t], x_in[:, u, t])
                    ins.then_inc(stat_step, 1)
                    dve_alone.wait_ge(stat_step, 3 * m + 1)
                    for t in range(TT):
                        ins = nc.vector.bn_aggr(mv[:, u, t], stats[:, u, t])
                    ins.then_inc(stat_step, 1)
                    dve.wait_ge(stat_step, 3 * m + 2)
                    if late(m, 2):
                        dve.wait_ge(xn_ready, m - 1)
                    nc.vector.tensor_scalar(veps[:, u], mv[:, u, :, 1], EPS, None, ALU.add).then_inc(var_ready, 1)
                    nc.vector.tensor_scalar(nmean[:, u], mv[:, u, :, 0], -1.0, None, ALU.mult).then_inc(stat_step, 1)
                    dve.wait_ge(std_ready, m + 1)
                    dve.wait_ge(stat_step, 3 * m + 3)
                    nc.vector.reciprocal(rstd[:, u], std[:, u]).then_inc(rstd_ready, 1)

                def split(b, c):
                    m, u = b * CB + c, c % 2
                    for k in range(5):
                        if k < 4:
                            dve.wait_ge(hi_ready, 4 * m + k + 1)
                            if late(m, 1):
                                dve.wait_ge(low_ready, 4 * m - 3 + k)
                            nc.vector.tensor_tensor(rest[:, k], qk32[:, u, k], parts[:, u, k, 0], ALU.subtract).then_inc(rest_ready, 1)
                        if k > 0:
                            dve.wait_ge(mid_ready, 4 * m + k)
                            nc.vector.tensor_tensor(parts[:, u, k - 1, 2], rest[:, k - 1], parts[:, u, k - 1, 1], ALU.subtract).then_inc(low_ready, 1)
                    if late(m, 2):
                        dve.wait_ge(v_stored[u], 16 * QB * turns(b, c))
                    for k in range(2):
                        dve.wait_ge(v_ready, 2 * m + k + 1)
                        for t in range(2 * k, 2 * k + 2):
                            ins = nc.vector.tensor_tensor(vp[:, u, t, :, 0:DH], psV[k][:, t % 2].rearrange("p (h w) -> p h w", h=H),
                                                          bv_sb[:].rearrange("p (h w) -> p h w", h=H), ALU.add)
                        ins.then_inc(v_out, 1)

                pipelined(dve, (statistics, 0), (split, 2))


STEPS = [(c, j) for c in range(CB) for j in range(TT * (c + 1))]
FIRST = [STEPS.index((c, 0)) for c in range(CB)] + [len(STEPS)]
NS = len(STEPS)
RING = 2
MW = 2 * CH


def row_maxima():
    for t in range(KT):
        for h in range(GH):
            keys = (t + 1) * P
            cuts = list(range(0, keys, MW)) + [keys]
            if (h, t) == (GH - 1, KT - 1):
                cuts.insert(1, CH)
            for slot, (k0, k1) in enumerate(zip(cuts, cuts[1:])):
                yield h, t, k0, k1 - k0, slot


MAXIMA = list(row_maxima())
NM = len(MAXIMA)
SLOTS = 3
USES = NM + 1 + CB
assert USES % RING == 0
M_FROM, M_TO, M_TURN = 0, 36, 37


def width(c, j):
    return CH - max(0, j - TT * c) * P


def ring_jobs(has_prev, has_next):
    jobs = [[] for _ in range(NS)]
    if has_prev:
        jobs[1].append(("z", CB - 1, True))
    for c in range(CB - 1):
        jobs[FIRST[c + 1] + 1].append(("z", c, False))
    if has_next:
        room = [width(*STEPS[s]) for s in range(M_FROM, M_TO)]
        cost = [64 + keys for _, _, _, keys, _ in MAXIMA]
        passed, given, spent = 0, 0, 0
        for s, w in zip(range(M_FROM, M_TO), room):
            passed += w
            while given < NM and (spent + cost[given] / 2) * sum(room) <= passed * sum(cost):
                jobs[s].append(("max", given))
                spent += cost[given]
                given += 1
        jobs[M_TURN].append(("turn",))
    return jobs


def ring_pair(n, k):
    first = {-1: 0, 0: NM + 1}.get(n, NM) if isinstance(n, int) else NM
    return (first + k) % RING


def ring_base(n):
    if isinstance(n, int) and n == 0:
        return NM + 1
    return USES * n + NM


def uses_to_z(n, c, has_next):
    if c == CB - 1:
        n, c, has_next = n + 1, -1, True
    jobs = [job for step in ring_jobs(True, has_next) for job in step]
    at = 0 if c < 0 else jobs.index(("z", c, False))
    return USES * n + NM + at + 1


def attend(nc, const, qk_scr, v_scr, zn_scr):
    ident, mask = const["ident"], const["mask"]
    with ExitStack() as ctx:
        sb = lambda name, shape, dt=F32: ctx.enter_context(nc.sbuf_tensor(name, shape, dt))
        sem = lambda name: ctx.enter_context(nc.semaphore(name))
        qs = [sb(f"qs{u}", [KMAX, GH, S], BF16) for u in range(3)]
        ks = [sb(f"ks{u}", [KMAX, GH, S], BF16) for u in range(3)]
        vq = [sb(f"vq{u}", [P, KT, GH, VW]) for u in range(3)]
        pr = [[sb(f"pr{p}{v}", [P, 2, CH]) for v in range(2)] for p in range(2)]
        mx = sb("mx", [P, GH, KT, SLOTS])
        negm = sb("negm", [P, P])
        mrest = sb("mrest", [GH * KT, P])
        mparts = sb("mparts", [GH * KT, PARTS, P], BF16)
        zt = [sb(f"zt{v}", [P, CH]) for v in range(2)]
        rl = sb("rl", [P, TT, GH])
        zn = [sb(f"zn{v}", [P, TT, GH, DH]) for v in range(2)]
        sc = [ctx.enter_context(nc.psum_tensor(f"sc{k}", [P, CH], F32)) for k in range(3)]
        ring = [ctx.enter_context(nc.psum_tensor(f"ring{k}", [P, MW], F32)) for k in range(RING)]
        pv = ctx.enter_context(nc.psum_tensor("pv", [P, CH], F32))

        qk_loaded = [sem(f"qk_loaded{u}") for u in range(3)]
        v_loaded = [sem(f"v_loaded{u}") for u in range(3)]
        set_up = sem("set_up")
        sc_ready = sem("sc_ready")
        exp_done = sem("exp_done")
        masked = sem("masked")
        pv_done = sem("pv_done")
        zt_done = sem("zt_done")
        ring_ready = sem("ring_ready")
        ring_done = sem("ring_done")
        negm_ready = sem("negm_ready")
        m_step = sem("m_step")
        m_landed = sem("m_landed")
        rl_ready = sem("rl_ready")
        zn_stored = [sem(f"zn_stored{u}") for u in range(2)]
        QKD = 16 * 2 * len(TERMS)
        DIAG = 2 * TT * CB

        def groups(eng, group):
            group(0, 0, 0, False, True)
            looped = (QUADS - 2) // 3
            with eng.Fori(0, looped) as i:
                group(3 * i + 1, i, 1, True, True)
                group(3 * i + 2, i, 2, True, True)
                group(3 * i + 3, i + 1, 0, True, True)
            for n in range(3 * looped + 1, QUADS):
                group(n, n // 3, n % 3, True, n + 1 < QUADS)

        def bank(n3, s, h):
            return (n3 * GH * NS + GH * s + h) % 3

        pool_tick, dve_tick, sp_tick = sem("pool_tick2"), sem("dve_tick2"), sem("sp_tick2")

        with nc.Block() as block:
            @block.sync
            def _(sp):
                sp_alone = Alone(sp, sp_tick)
                def load_qk(n, u):
                    for w, dst in ((0, qs[u]), (1, ks[u])):
                        rows = qk_scr[w].rearrange("s b (g h d) t -> s (b g) d h t", g=QB, d=DH)
                        for i, term in enumerate(TERMS):
                            sp.dma_start(dst[DH * i:DH * (i + 1), :, :], rows[term[w], n]).then_inc(qk_loaded[u], 16)

                def load_v(n, u):
                    sp.dma_start(vq[u][:].rearrange("p j h w -> p j (h w)"),
                                 v_scr.rearrange("b g p j w -> (b g) p j w")[n]).then_inc(v_loaded[u], 16)

                def put_maxima(done, u):
                    sp_alone.wait_ge(ring_done, done)
                    for s in range(PARTS):
                        sp.dma_start(qs[u][KROWS + s:KROWS + s + 1, :, :], mparts[:, s, :]).then_inc(m_landed, 16)

                def store_z(n, c, done):
                    sp_alone.wait_ge(ring_done, done)
                    sp.dma_start(zn_scr[n, c], zn[c % 2][:].rearrange("p t h d -> p t (h d)")).then_inc(zn_stored[c % 2], 16)

                def group(n, r, u, has_prev, has_next):
                    if has_prev:
                        sp.wait_ge(pv_done, NS * n)
                    if not isinstance(n, int) or n + 2 < QUADS:
                        load_qk(n + 2, (u + 2) % 3)
                        load_v(n + 2, (u + 2) % 3)
                    done = ring_base(n)
                    for jobs in ring_jobs(has_prev, has_next):
                        for job in jobs:
                            done = done + 1
                            if job[0] == "z":
                                store_z(n - 1 if job[2] else n, job[1], done)
                            if job[0] == "turn":
                                put_maxima(done, (u + 1) % 3)
                    if not has_next:
                        store_z(n, CB - 1, done + 1)

                load_qk(0, 0)
                load_v(0, 0)
                load_qk(1, 1)
                load_v(1, 1)
                put_maxima(NM + 1, 0)
                groups(sp, group)
                for u in range(2):
                    sp.wait_ge(zn_stored[u], 16 * CB * QUADS // 2)

            @block.gpsimd
            def _(pool):
                pool_alone = Alone(pool, pool_tick)
                def group(n, r, u, has_prev, has_next):
                    for s, (c, j) in enumerate(STEPS):
                        q0 = CH - width(c, j)
                        if j < TT * c:
                            continue
                        for p in range(2):
                            pool_alone.wait_ge(exp_done, GH * (NS * n + s) + 2 * p + 2)
                            tile = pr[p][s % 2][:, :, q0:q0 + P]
                            nc.gpsimd.affine_select(out=tile, in_=tile, compare_op=ALU.is_ge, fill=0.0, base=0,
                                                    pattern=[[0, 2], [1, P]], channel_multiplier=-1).then_inc(masked, 1)

                groups(pool, group)

            @block.scalar
            def _(act):
                def z_out(n, c, has_next):
                    g = CB * n + c
                    act.wait_ge(pv_done, NS * n + FIRST[c + 1])
                    if late(g, 2):
                        act.wait_ge(ring_done, uses_to_z(n, c - 2, has_next) if c >= 2 else uses_to_z(n - 1, c + CB - 2, True))
                    nc.scalar.activation(zt[c % 2][:], pv[:], ACT.Copy).then_inc(zt_done, 1)

                def group(n, r, u, has_prev, has_next):
                    for s, (c, j) in enumerate(STEPS):
                        q0 = CH - width(c, j)
                        for h in range(GH):
                            act.wait_ge(sc_ready, GH * (NS * n + s) + h + 1)
                            if h == 0 and (has_prev or s >= 2):
                                act.wait_ge(pv_done, NS * n + s - 1)
                            nc.scalar.activation(pr[h // 2][s % 2][:, h % 2, q0:], sc[bank(u, s, h)][:, q0:], ACT.Exp).then_inc(exp_done, 1)
                        if j == 0 and c > 0:
                            z_out(n, c - 1, has_next)
                        if s == 0 and has_prev:
                            z_out(n - 1, CB - 1, True)

                groups(act, group)
                z_out(QUADS - 1, CB - 1, False)

            @block.tensor
            def _(pe):
                def ring_job(job, base, k, n, to):
                    if k >= RING:
                        pe.wait_ge(ring_done, base + k - RING + 1)
                    elif not (isinstance(base, int) and base == 0):
                        pe.wait_ge(ring_done, base)
                    pair = ring[ring_pair(n, k)]
                    if job[0] == "max":
                        h, t, k0, keys, _ = MAXIMA[job[1]]
                        for k1 in range(0, keys, CH):
                            w = min(CH, keys - k1)
                            ins = pe.matmul(pair[:, k1:k1 + w], qs[to][0:KROWS, h, t * P:(t + 1) * P], ks[to][0:KROWS, h, k0 + k1:k0 + k1 + w],
                                            start=True, stop=True)
                        ins.then_inc(ring_ready, 1)
                    if job[0] == "turn":
                        pe.wait_ge(negm_ready, n + 2)
                        pe.transpose(pair[:, 0:P], negm[:], ident[:]).then_inc(ring_ready, 1)
                    if job[0] == "z":
                        c = job[1]
                        pe.wait_ge(zt_done, CB * (n - 1 if job[2] else n) + c + 1)
                        for t in range(TT):
                            ins = pe.transpose(pair[:, t * P:(t + 1) * P], zt[c % 2][:, t * P:(t + 1) * P], ident[:])
                        ins.then_inc(ring_ready, 1)

                def scores(n, u, s, h):
                    c, j = STEPS[s]
                    q0 = CH - width(c, j)
                    if s > 0 or h > 2 or not (isinstance(n, int) and n == 0):
                        pe.wait_ge(exp_done, GH * (NS * n + s) + h - 2)
                    pe.matmul(sc[bank(u, s, h)][:, q0:], ks[u][:, h, j * P:(j + 1) * P], qs[u][:, h, c * CH + q0:(c + 1) * CH],
                              start=True, stop=True).then_inc(sc_ready, 1)

                def values(n, r, u, s):
                    c, j = STEPS[s]
                    q0 = CH - width(c, j)
                    if j == 0:
                        pe.wait_ge(v_loaded[u], 16 * (r + 1))
                        if c > 0 or not (isinstance(n, int) and n == 0):
                            pe.wait_ge(zt_done, CB * n + c)
                    if j >= TT * c:
                        pe.wait_ge(masked, DIAG * n + 2 * j + 2)
                    else:
                        pe.wait_ge(exp_done, GH * (NS * n + s + 1))
                    for h in range(GH):
                        ins = pe.matmul(pv[VW * h:VW * (h + 1), q0:], vq[u][:, j, h], pr[h // 2][s % 2][:, h % 2, q0:],
                                        start=j == 0, stop=j == TT * (c + 1) - 1)
                    ins.then_inc(pv_done, 1)

                def group(n, r, u, has_prev, has_next):
                    base, k = ring_base(n), 0
                    pe.wait_ge(m_landed, 16 * PARTS * (n + 1))
                    if has_next:
                        pe.wait_ge(qk_loaded[(u + 1) % 3], QKD * (r + (u + 1) // 3 + 1))
                    for s, jobs in enumerate(ring_jobs(has_prev, has_next)):
                        for part in range(3):
                            if part < 2:
                                scores(n, u, s, 2 * part)
                                scores(n, u, s, 2 * part + 1)
                            elif s > 0:
                                values(n, r, u, s - 1)
                            elif has_prev:
                                values(n - 1, r if u else r - 1, (u + 2) % 3, NS - 1)
                            for job in jobs[(part * len(jobs) + 2) // 3:((part + 1) * len(jobs) + 2) // 3]:
                                ring_job(job, base, k, n, (u + 1) % 3)
                                k += 1

                pe.wait_ge(qk_loaded[0], QKD)
                pe.wait_ge(set_up, 5)
                for k in range(NM):
                    ring_job(("max", k), 0, k, -1, 0)
                ring_job(("turn",), 0, NM, -1, 0)
                groups(pe, group)
                values(QUADS - 1, (QUADS - 1) // 3, (QUADS - 1) % 3, NS - 1)
                ring_job(("z", CB - 1, False), ring_base(QUADS - 1), CB, QUADS - 1, 0)

            @block.vector
            def _(dve):
                dve_alone = Alone(dve, dve_tick)
                def ring_job(job, done, n, bank, m_before):
                    if job[0] != "max":
                        dve.wait_ge(ring_done, done)
                    if job[0] == "turn":
                        nc.vector.tensor_reduce(negm[:, 0:GH * KT], mx[:].rearrange("p h t k -> p (h t) k"), AX.X, ALU.max,
                                                negate=True).then_inc(negm_ready, 1)
                    dve_alone.wait_ge(ring_ready, done + 1)
                    if job[0] == "max":
                        h, t, k0, keys, slot = MAXIMA[job[1]]
                        to = mx[:, h, t, slot:slot + 1]
                        if job[1] == 0:
                            if m_before:
                                dve_alone.wait_ge(negm_ready, n + 1)
                        if k0 + keys < (t + 1) * P:
                            nc.vector.tensor_reduce(to, bank[:, 0:keys], AX.X, ALU.max).then_inc(ring_done, 1)
                        else:
                            nc.vector.tensor_tensor_reduce(out=bank[:, 0:keys], in0=bank[:, 0:keys], in1=mask[:, MW - keys:MW], scale=1.0,
                                                           scalar=NEG, op0=ALU.add, op1=ALU.max, accum_out=to).then_inc(ring_done, 1)
                    if job[0] == "turn":
                        if m_before:
                            dve.wait_ge(m_landed, 16 * PARTS * (n + 1))
                        rows = bank[0:GH * KT, 0:P]
                        base = 3 * (n + 1)
                        nc.vector.tensor_copy(mparts[:, 0], rows).then_inc(m_step, 1)
                        dve.wait_ge(m_step, base + 1)
                        nc.vector.tensor_tensor(mrest[:], rows, mparts[:, 0], ALU.subtract).then_inc(m_step, 1)
                        dve.wait_ge(m_step, base + 2)
                        nc.vector.tensor_copy(mparts[:, 1], mrest[:]).then_inc(m_step, 1)
                        dve.wait_ge(m_step, base + 3)
                        nc.vector.tensor_tensor(mparts[:, 2], mrest[:], mparts[:, 1], ALU.subtract).then_inc(ring_done, 1)
                    if job[0] == "z":
                        nn, c = (n - 1 if job[2] else n), job[1]
                        g = CB * nn + c
                        z = bank[:, 0:CH].rearrange("p (t h w) -> p t h w", t=TT, h=GH)
                        nc.vector.reciprocal(rl[:], z[:, :, :, DH]).then_inc(rl_ready, 1)
                        dve.wait_ge(rl_ready, g + 1)
                        if late(g, 2):
                            dve.wait_ge(zn_stored[c % 2], 16 * turns(nn, c))
                        nc.vector.tensor_tensor(zn[c % 2][:], z[:, :, :, 0:DH], rl[:].unsqueeze(3).broadcast_to([P, TT, GH, DH]),
                                                ALU.mult).then_inc(ring_done, 1)

                def group(n, r, u, has_prev, has_next):
                    base, k = ring_base(n), 0
                    for jobs in ring_jobs(has_prev, has_next):
                        for job in jobs:
                            ring_job(job, base + k, n, ring[ring_pair(n, k)], True)
                            k += 1

                for u in range(3):
                    nc.vector.memset(ks[u][KROWS:KMAX], 1.0).then_inc(set_up, 1)
                nc.vector.memset(mx[:], NEG).then_inc(set_up, 1)
                nc.vector.memset(negm[:], 0.0).then_inc(set_up, 1)

                dve.wait_ge(set_up, 5)
                for k in range(NM):
                    ring_job(("max", k), k, -1, ring[ring_pair(-1, k)], False)
                ring_job(("turn",), NM, -1, ring[ring_pair(-1, NM)], False)
                groups(dve, group)
                ring_job(("z", CB - 1, False), ring_base(QUADS - 1) + CB, QUADS - 1, ring[ring_pair(QUADS - 1, CB)], True)


HT = HID // P
HB = 4
ZR = DH + 2


def feed(nc, const, x, W1T, b1, W2T, b2, WO, bO, scale, xnT_scr, lt_scr, zn_scr, out):
    ident = const["ident"]
    with ExitStack() as ctx:
        sb = lambda name, shape, dt=F32: ctx.enter_context(nc.sbuf_tensor(name, shape, dt))
        sem = lambda name: ctx.enter_context(nc.semaphore(name))
        w1t = sb("w1t", [P, KD, HID])
        w2t = sb("w2t", [P, HT, D])
        next1 = sb("next1", [P, KD, HID])
        next2 = sb("next2", [P, HT, D])
        eff1 = sb("eff1", [P, KD, HID])
        eff2 = sb("eff2", [P, HT, D])
        b1c = sb("b1c", [P, HT])
        wo = sb("wo", [ZR, D])
        scale_c = sb("scale_c", [P, 1])
        even = sb("even", [P, 2 * RANKS, D])
        first = sb("first", [P, KD, LORA + 4])
        odd = sb("odd", [P, KD, 2 * RANKS])
        xc = [sb(f"xc{u}", [P, KD, CH]) for u in range(2)]
        x_res = [sb(f"x_res{u}", [P, TT, D]) for u in range(2)]
        zn_in = [sb(f"zn_in{u}", [P, QB, TT, GH * DH]) for u in range(2)]
        zs = [sb(f"zs{u}", [P, TT, ZR]) for u in range(2)]
        zT = [sb(f"zT{u}", [ZR, CH]) for u in range(2)]
        g = [sb(f"g{u}", [P, HT, CH]) for u in range(2)]
        y = [sb(f"y{u}", [P, TT, D]) for u in range(2)]
        ps_h = [ctx.enter_context(nc.psum_tensor(f"ps_h{k}", [P, CH], F32)) for k in range(HB)]
        ps_y = [ctx.enter_context(nc.psum_tensor(f"ps_y{k}", [P, CH], F32)) for k in range(2)]
        ps_z = ctx.enter_context(nc.psum_tensor("ps_z", [P, CH], F32))

        w_loaded = sem("feed_w_loaded")
        scale_loaded = sem("feed_scale")
        ones_set = sem("feed_ones_set")
        first_loaded = sem("feed_first")
        odd_ready = sem("feed_odd_ready")
        outer = sem("feed_outer")
        next_ready = sem("feed_next_ready")
        eff1_ready = sem("feed_eff1_ready")
        eff2_ready = sem("feed_eff2_ready")
        xc_loaded = [sem(f"feed_xc_loaded{u}") for u in range(2)]
        x_loaded = [sem(f"feed_x_loaded{u}") for u in range(2)]
        z_loaded = [sem(f"feed_z_loaded{u}") for u in range(2)]
        zs_ready = sem("feed_zs_ready")
        z_turned = sem("feed_z_turned")
        zT_ready = sem("feed_zT_ready")
        h_ready = sem("feed_h_ready")
        g_ready = sem("feed_g_ready")
        y_made = sem("feed_y_made")
        y_ready = sem("feed_y_ready")
        y_stored = [sem(f"feed_y_stored{u}") for u in range(2)]
        W_DMAS = 6

        pool_tick = sem("pool_tick3")

        with nc.Block() as block:
            @block.sync
            def _(sp):
                sp.dma_start(w1t[:], W1T.rearrange("(c p) h -> p c h", p=P)).then_inc(w_loaded, 16)
                sp.dma_start(w2t[:], W2T.rearrange("(c p) o -> p c o", p=P)).then_inc(w_loaded, 16)
                sp.dma_start(b1c[:], b1.rearrange("(c p) -> p c", p=P), allow_slow_non_contiguous=True).then_inc(w_loaded, 16)
                sp.dma_start(wo[0:DH], WO).then_inc(w_loaded, 16)
                sp.dma_start(wo[DH:DH + 1], bO.rearrange("(a n) -> a n", a=1)).then_inc(w_loaded, 16)
                sp.dma_start(wo[DH + 1:DH + 2], b2.rearrange("(a n) -> a n", a=1)).then_inc(w_loaded, 16)

                def load(b, c):
                    m, u = b * CB + c, c % 2
                    if late(m, 2):
                        sp.wait_ge(h_ready, HT * (m - 1))
                    sp.dma_start(xc[u][:], xnT_scr[m]).then_inc(xc_loaded[u], 16)
                    if late(m, 2):
                        sp.wait_ge(zs_ready, m - 1)
                    sp.dma_start(zn_in[u][:].rearrange("p q t w -> p q (t w)"),
                                 zn_scr.rearrange("(b q) c p t w -> b c p q (t w)", q=QB)[b, c]).then_inc(z_loaded[u], 16)
                    if late(m, 2):
                        sp.wait_ge(y_ready, TT * (m - 1))
                    sp.dma_start(x_res[u][:], x[b, c * CH:(c + 1) * CH, :].rearrange("(t p) d -> p t d", p=P)).then_inc(x_loaded[u], 16)

                def store(b, c):
                    m, u = b * CB + c, c % 2
                    sp.wait_ge(y_ready, TT * (m + 1))
                    sp.dma_start(out[b, c * CH:(c + 1) * CH, :].rearrange("(t p) d -> p t d", p=P), y[u][:]).then_inc(y_stored[u], 16)

                pipelined(sp, (load, 0), (store, 2))
                for u in range(2):
                    sp.wait_ge(y_stored[u], 16 * NCH // 2)

            @block.gpsimd
            def _(pool):
                pool_alone = Alone(pool, pool_tick)
                pool.dma_start(scale_c[:], scale.broadcast_to([P, 1])).then_inc(scale_loaded, 16)
                for u in range(2):
                    nc.gpsimd.memset(zs[u][:, :, DH:DH + 1], float(H)).then_inc(ones_set, 1)
                    nc.gpsimd.memset(zs[u][:, :, DH + 1:DH + 2], 1.0).then_inc(ones_set, 1)
                pool.wait_ge(scale_loaded, 16)
                pool.wait_ge(w_loaded, 16 * W_DMAS)

                def prepare(b):
                    if late(b, 1):
                        pool_alone.wait_ge(outer, 2 * b)
                    pool.dma_start(even[:], lt_scr[b * CB].rearrange("(i two) d -> two i d", two=2)[0:1].broadcast_to([P, 2 * RANKS, D])
                                   ).then_inc(first_loaded, 16)
                    pool.dma_start(first[:], xnT_scr[b * CB][:, :, 0:LORA + 4]).then_inc(first_loaded, 16)
                    pool_alone.wait_ge(first_loaded, 32 * (b + 1))
                    nc.gpsimd.tensor_scalar(odd[:], first[:, :, 2:2 + LORA:2], scale_c[:, 0:1], None, ALU.mult).then_inc(odd_ready, 1)
                    pool_alone.wait_ge(odd_ready, b + 1)
                    if late(b, 1):
                        pool_alone.wait_ge(eff1_ready, b)
                    for c in range(KD):
                        for i in range(RANKS):
                            ins = nc.gpsimd.tensor_scalar(next1[:, c, D * i:D * (i + 1)], even[:, i], odd[:, c, i:i + 1], 1.0, ALU.mult, ALU.mult)
                    ins.then_inc(outer, 1)
                    if late(b, 1):
                        pool_alone.wait_ge(eff2_ready, b)
                    for k in range(HT):
                        for i in range(RANKS):
                            w = D // RANKS
                            ins = nc.gpsimd.tensor_scalar(next2[:, k, w * i:w * (i + 1)], even[:, RANKS + i, k // KD::RANKS],
                                                          odd[:, k % KD, RANKS + i:RANKS + i + 1], 1.0, ALU.mult, ALU.mult)
                    ins.then_inc(outer, 1)
                    pool_alone.wait_ge(outer, 2 * b + 2)
                    nc.gpsimd.tensor_tensor(next1[:], next1[:], w1t[:], ALU.add).then_inc(next_ready, 1)
                    nc.gpsimd.tensor_tensor(next2[:], next2[:], w2t[:], ALU.add).then_inc(next_ready, 1)

                prepare(0)
                with pool.Fori(1, B) as b:
                    prepare(b)

            @block.scalar
            def _(act):
                act.wait_ge(w_loaded, 16 * W_DMAS)

                def gelu(b, c):
                    m, u = b * CB + c, c % 2
                    act.wait_ge(z_turned, m + 1)
                    if late(m, 2):
                        act.wait_ge(y_made, TT * (m - 1))
                    nc.scalar.activation(zT[u][:], ps_z[0:ZR], ACT.Identity).then_inc(zT_ready, 1)
                    for k in range(HT):
                        act.wait_ge(h_ready, HT * m + k + 1)
                        nc.scalar.activation(g[u][:, k], ps_h[k % HB][:], ACT.Gelu, bias=b1c[:, k:k + 1]).then_inc(g_ready, 1)

                pipelined(act, (gelu, 0))

            @block.tensor
            def _(pe):
                pe.wait_ge(w_loaded, 16 * W_DMAS)

                def hidden(b, c):
                    m, u = b * CB + c, c % 2
                    pe.wait_ge(zs_ready, m + 1)
                    if late(m, 1):
                        pe.wait_ge(zT_ready, m)
                    for t in range(TT):
                        ins = pe.transpose(ps_z[0:ZR, t * P:(t + 1) * P], zs[u][:, t], ident[:])
                    ins.then_inc(z_turned, 1)
                    pe.wait_ge(xc_loaded[u], 16 * (turns(b, c) + 1))
                    if c == 0:
                        pe.wait_ge(eff1_ready, b + 1)
                    for k in range(HT):
                        if late(m, 1) or k >= HB:
                            pe.wait_ge(g_ready, HT * m + k - HB + 1)
                        for d in range(KD):
                            ins = pe.matmul(ps_h[k % HB][:], eff1[:, d, k * P:(k + 1) * P], xc[u][:, d], start=d == 0, stop=d == KD - 1)
                        ins.then_inc(h_ready, 1)

                def outputs(b, c):
                    m, u = b * CB + c, c % 2
                    pe.wait_ge(g_ready, HT * (m + 1))
                    pe.wait_ge(zT_ready, m + 1)
                    if c == 0:
                        pe.wait_ge(eff2_ready, b + 1)
                    for t in range(TT):
                        if late(m, 1) or t >= 2:
                            pe.wait_ge(y_ready, TT * m + t - 1)
                        to = ps_y[t % 2][:, 0:D]
                        pe.matmul(to, zT[u][:, t * P:(t + 1) * P], wo[:], start=True, stop=False)
                        for k in range(HT):
                            ins = pe.matmul(to, g[u][:, k, t * P:(t + 1) * P], eff2[:, k], start=False, stop=k == HT - 1)
                        ins.then_inc(y_made, 1)

                pipelined(pe, (hidden, 0), (outputs, 1))

            @block.vector
            def _(dve):
                dve.wait_ge(ones_set, 4)

                def gather(b, c):
                    m, u = b * CB + c, c % 2
                    dve.wait_ge(z_loaded[u], 16 * (turns(b, c) + 1))
                    if late(m, 2):
                        dve.wait_ge(z_turned, m - 1)
                    for t in range(TT):
                        ins = nc.vector.tensor_reduce(zs[u][:, t, 0:DH], zn_in[u][:, :, t].rearrange("p q (h d) -> p d q h", d=DH), AX.XY, ALU.add)
                    ins.then_inc(zs_ready, 1)
                    if c == 0:
                        dve.wait_ge(next_ready, 2 * b + 2)
                        if late(b, 1):
                            dve.wait_ge(h_ready, HT * m)
                        nc.vector.tensor_copy(eff1[:], next1[:]).then_inc(eff1_ready, 1)
                    if c == 1:
                        if late(b, 1):
                            dve.wait_ge(y_made, TT * (m - 1))
                        nc.vector.tensor_copy(eff2[:], next2[:]).then_inc(eff2_ready, 1)

                def finish(b, c):
                    m, u = b * CB + c, c % 2
                    dve.wait_ge(x_loaded[u], 16 * (turns(b, c) + 1))
                    if late(m, 2):
                        dve.wait_ge(y_stored[u], 16 * turns(b, c))
                    for t in range(TT):
                        dve.wait_ge(y_made, TT * m + t + 1)
                        nc.vector.tensor_tensor(y[u][:, t], ps_y[t % 2][:, 0:D], x_res[u][:, t], ALU.add).then_inc(y_ready, 1)

                pipelined(dve, (gather, 0), (finish, 1))


def program(nc, x, WQ, bQ, WK, bK, WV, bV, WO, bO, W1T, b1, W2T, b2, scale, out):
    scr = lambda name, shape, dt=F32: nc.dram_tensor(name, shape, dt, kind="Internal").ap()
    qk_scr = scr("qk_scr", [2, PARTS, B, D, S], BF16)
    v_scr = scr("v_scr", [B, QB, P, KT, GH * VW])
    xnT_scr = scr("xnT_scr", [NCH, P, KD, CH])
    lt_scr = scr("lt_scr", [NCH, LORA, D])
    zn_scr = scr("zn_scr", [QUADS, CB, P, TT, GH * DH])
    with ExitStack() as ctx:
        const = {
            "ident": ctx.enter_context(nc.sbuf_tensor("ident", [P, P], F32)),
            "mask": ctx.enter_context(nc.sbuf_tensor("mask", [P, 2 * CH], F32)),
        }
        project(nc, const, x, WQ, bQ, WK, bK, WV, bV, qk_scr, v_scr, xnT_scr, lt_scr)
        attend(nc, const, qk_scr, v_scr, zn_scr)
        feed(nc, const, x, W1T, b1, W2T, b2, WO, bO, scale, xnT_scr, lt_scr, zn_scr, out)


def kernel(**inputs):
    import numpy as np
    import concourse.bacc as bacc
    from concourse.bass_utils import run_bass_kernel_spmd

    a = {k.removeprefix("L0_attn_").removeprefix("L0_ffn_"): np.asarray(v) for k, v in inputs.items()}
    arrays = {
        "x": a["x"], "WQ": a["WQ"], "bQ": a["bQ"], "WK": a["WK"], "bK": a["bK"], "WV": a["WV"], "bV": a["bV"],
        "WO": a["WO"], "bO": a["bO"], "W1T": a["W1"].T, "b1": a["b1"], "W2T": a["W2"].T, "b2": a["b2"],
        "scale": a["scale"].reshape(1, 1),
    }
    nc = bacc.Bacc("TRN2", target_bir_lowering=False, num_devices=1)
    given, aps = {}, []
    for name, v in arrays.items():
        v = np.ascontiguousarray(v)
        given[f"in_{name}"] = v
        aps.append(nc.dram_tensor(f"in_{name}", v.shape, mybir.dt.from_np(v.dtype), kind="ExternalInput").ap())
    out = nc.dram_tensor("out_y", (B, S, D), F32, kind="ExternalOutput").ap()
    program(nc, *aps, out)
    r = run_bass_kernel_spmd(nc, [given], core_ids=[0])
    return r.results[0]["out_y"]
```

```python
from contextlib import ExitStack

import concourse.bass as bass
from concourse import mybir
from concourse.alu_op_type import AluOpType as ALU

ACT = mybir.ActivationFunctionType
AX = mybir.AxisListType
F32 = mybir.dt.float32
BF16 = mybir.dt.bfloat16

P = 128
B, S, D, H = 4, 2048, 256, 16
DH = D // H
HID = 1024
TOK = B * S
KD = D // P
CH = 512
CB = S // CH
NCH = TOK // CH
TT = CH // P
GH = 4
QUADS = B * H // GH
QB = H // GH
KT = S // P
VW = 32
PARTS = 3
TERMS = [(0, 0), (0, 1), (1, 0), (1, 1), (0, 2), (2, 0)]
KROWS = len(TERMS) * DH
KMAX = KROWS + PARTS
EPS = 1e-5
NEG = -1e30
LORA = 16
RANKS = 4


def late(m, k):
    return not isinstance(m, int) or m >= k


def turns(b, c):
    return b * (CB // 2) + c // 2


class Alone:

    def __init__(self, eng, tick):
        self.eng, self.tick = eng, tick

    def wait_ge(self, sem, value):
        self.eng.wait_ge(sem, value)
        if not isinstance(value, int):
            self.eng.sem_inc(self.tick, 1)


def pipelined(eng, *stages, before_last=None):
    def steps(b):
        for c in range(CB):
            for stage, lag in stages:
                if b is None:
                    if c >= lag:
                        stage(0, c - lag)
                else:
                    stage(b if c >= lag else b - 1, (c - lag) % CB)

    steps(None)
    with eng.Fori(1, B) as b:
        steps(b)
    if before_last:
        before_last()
    for k in range(1, CB):
        for stage, lag in stages:
            if k <= lag:
                stage(B - 1, CB - 1 - lag + k)


def project(nc, const, x, WQ, bQ, WK, bK, WV, bV, qk_scr, v_scr, xnT_scr, lt_scr, group0, stored):
    ident = const["ident"]
    with ExitStack() as ctx:
        sb = lambda name, shape, dt=F32: ctx.enter_context(nc.sbuf_tensor(name, shape, dt))
        sem = lambda name: ctx.enter_context(nc.semaphore(name))
        w_sb = sb("w_sb", [P, 3, KD, D])
        b_in = sb("b_in", [P, 2, 2])
        b_sb = sb("b_sb", [P, 2, 2])
        bv_sb = sb("bv_sb", [P, D])
        x_in = sb("x_in", [P, 2, TT, D])
        xn = sb("xn", [P, 2, TT, D])
        xnT = sb("xnT", [P, 2, KD, CH])
        stats = sb("stats", [P, 2, TT, 6])
        mv = sb("mv", [P, 2, TT, 2])
        veps = sb("veps", [P, 2, TT])
        nmean = sb("nmean", [P, 2, TT])
        std = sb("std", [P, 2, TT])
        rstd = sb("rstd", [P, 2, TT])
        qk32 = sb("qk32", [P, 2, 4, CH])
        parts = sb("parts", [P, 2, 4, PARTS, CH], BF16)
        rest = sb("rest", [P, 4, CH])
        vp = sb("vp", [P, 2, TT, H, VW])
        psT = [ctx.enter_context(nc.psum_tensor(f"psT{d}", [P, CH], F32)) for d in range(KD)]
        psQK = [ctx.enter_context(nc.psum_tensor(f"psQK{k}", [P, CH], F32)) for k in range(4)]
        psV = [ctx.enter_context(nc.psum_tensor(f"psV{k}", [P, 2, D], F32)) for k in range(2)]

        w_loaded = sem("w_loaded")
        x_loaded = [sem(f"x_loaded{u}") for u in range(2)]
        const_ready = sem("const_ready")
        bias_ready = sem("bias_ready")
        stat_step = sem("stat_step")
        var_ready = sem("var_ready")
        std_ready = sem("std_ready")
        rstd_ready = sem("rstd_ready")
        xn_ready = sem("xn_ready")
        xT_ready = sem("xT_ready")
        xnT_ready = sem("xnT_ready")
        qk_ready = sem("qk_ready")
        qk_out = sem("qk_out")
        hi_ready = sem("hi_ready")
        rest_ready = sem("rest_ready")
        low_ready = sem("low_ready")
        v_ready = sem("v_ready")
        v_out = sem("v_out")
        mid_ready = sem("mid_ready")
        lt_stored, xnT_stored, qk_stored, v_stored = stored

        W_DMAS = 3 + 2 + 1

        pool_tick, dve_tick, sp_tick = sem("pool_tick1"), sem("dve_tick1"), sem("sp_tick1")

        with nc.Block() as block:
            @block.sync
            def _(sp):
                sp_alone = Alone(sp, sp_tick)
                def load(b, c):
                    m = b * CB + c
                    if late(m, 2):
                        sp.wait_ge(xn_ready, m - 1)
                    sp.dma_start(x_in[:, c % 2], x[b, c * CH:(c + 1) * CH, :].rearrange("(t p) d -> p t d", p=P)).then_inc(x_loaded[c % 2], 16)

                def store_norm(b, c):
                    m, u = b * CB + c, c % 2
                    sp.wait_ge(xn_ready, m + 1)
                    sp.dma_start(lt_scr[m], xn[1:1 + LORA, u, 0, :]).then_inc(lt_stored[u], 16)
                    sp.wait_ge(xnT_ready, m + 1)
                    sp.dma_start(xnT_scr[m], xnT[:, u]).then_inc(xnT_stored[u], 16)

                def store_qkv(b, c):
                    m, u = b * CB + c, c % 2
                    sp_alone.wait_ge(low_ready, 4 * (m + 1))
                    for k in range(4):
                        sp.dma_start(qk_scr[k // 2, :, b, P * (k % 2):P * (k % 2 + 1), c * CH:(c + 1) * CH].rearrange("s r t -> r s t"),
                                     parts[:, u, k]).then_inc(qk_stored[u], 16)
                    sp.wait_ge(v_out, 2 * m + 2)
                    for g in range(QB):
                        sp.dma_start(v_scr[b, g, :, c * TT:(c + 1) * TT, :],
                                     vp[:, u, :, GH * g:GH * (g + 1)].rearrange("p t h w -> p t (h w)")).then_inc(v_stored[u], 16)

                def load_group0():
                    for u in range(2):
                        sp.wait_ge(qk_stored[u], 16 * 4 * turns(B - 1, 2 - u))
                    load_qk(sp, qk_scr, 0, group0)

                pipelined(sp, (load, 0), (store_norm, 2), (store_qkv, 3), before_last=load_group0)

            @block.gpsimd
            def _(pool):
                pool_alone = Alone(pool, pool_tick)
                nc.gpsimd.memset(ident[:], 0.0).then_inc(const_ready, 1)
                nc.gpsimd.memset(const["mask"][:], 0.0).then_inc(const_ready, 1)
                nc.gpsimd.memset(vp[:], 0.0).then_inc(const_ready, 1)
                nc.gpsimd.memset(const["ones"][:], 1.0).then_inc(const_ready, 1)
                pool.wait_ge(const_ready, 4)
                nc.gpsimd.affine_select(out=ident[:], in_=ident[:], compare_op=ALU.not_equal, fill=1.0, base=0,
                                        pattern=[[-1, P]], channel_multiplier=1).then_inc(const_ready, 1)
                nc.gpsimd.affine_select(out=const["mask"][:, 2 * CH - P:], in_=const["mask"][:, 2 * CH - P:], compare_op=ALU.is_ge,
                                        fill=NEG, base=0, pattern=[[-1, P]], channel_multiplier=1).then_inc(const_ready, 1)
                nc.gpsimd.memset(vp[:, :, :, :, DH:DH + 1], 1.0).then_inc(const_ready, 1)

                def norm(b, c):
                    m, u = b * CB + c, c % 2
                    pool_alone.wait_ge(rstd_ready, m + 1)
                    if late(m, 2):
                        pool_alone.wait_ge(xT_ready, m - 1)
                        pool_alone.wait_ge(lt_stored[u], 16 * turns(b, c))
                    for t in range(TT):
                        ins = nc.gpsimd.tensor_scalar(xn[:, u, t], x_in[:, u, t], nmean[:, u, t:t + 1], rstd[:, u, t:t + 1],
                                                      ALU.add, ALU.mult)
                    ins.then_inc(xn_ready, 1)

                def high(b, c):
                    m, u = b * CB + c, c % 2
                    if late(m, 2):
                        pool_alone.wait_ge(qk_stored[u], 16 * 4 * turns(b, c))
                    for k in range(4):
                        pool_alone.wait_ge(qk_out, 4 * m + k + 1)
                        nc.gpsimd.tensor_scalar(parts[:, u, k, 0], qk32[:, u, k], 1.0, 0.0, ALU.mult, ALU.add).then_inc(hi_ready, 1)

                pipelined(pool, (high, 2), (norm, 0))

            @block.scalar
            def _(act):
                for k, w in enumerate((WQ, WK, WV)):
                    act.dma_start(w_sb[:, k], w.rearrange("(c p) n -> p c n", p=P)).then_inc(w_loaded, 16)
                for k, b in enumerate((bQ, bK)):
                    act.dma_start(b_in[:, k], b.rearrange("(g p) -> p g", p=P), allow_slow_non_contiguous=True).then_inc(w_loaded, 16)
                act.dma_start(bv_sb[:, :], bV.rearrange("(a n) -> a n", a=1).broadcast_to([P, D])).then_inc(w_loaded, 16)
                act.wait_ge(w_loaded, 16 * W_DMAS)
                nc.scalar.activation(b_sb[:, 0], b_in[:, 0], ACT.Identity, scale=0.25).then_inc(bias_ready, 1)
                nc.scalar.activation(b_sb[:, 1], b_in[:, 1], ACT.Identity).then_inc(bias_ready, 1)
                act.wait_ge(bias_ready, 2)

                def root(b, c):
                    m, u = b * CB + c, c % 2
                    act.wait_ge(var_ready, m + 1)
                    nc.scalar.activation(std[:, u], veps[:, u], ACT.Sqrt).then_inc(std_ready, 1)

                def turn(b, c):
                    m, u = b * CB + c, c % 2
                    act.wait_ge(xT_ready, m + 1)
                    if late(m, 2):
                        act.wait_ge(v_ready, 2 * (m - 1))
                        act.wait_ge(xnT_stored[u], 16 * turns(b, c))
                    for d in range(KD):
                        ins = nc.scalar.activation(xnT[:, u, d], psT[d][:], ACT.Identity)
                    ins.then_inc(xnT_ready, 1)

                def out(b, c):
                    m, u = b * CB + c, c % 2
                    if late(m, 2):
                        act.wait_ge(rest_ready, 4 * (m - 1))
                    for k in range(5):
                        if k < 4:
                            act.wait_ge(qk_ready, 4 * m + k + 1)
                            nc.scalar.activation(qk32[:, u, k], psQK[k][:], ACT.Identity, bias=b_sb[:, k // 2, k % 2:k % 2 + 1],
                                                 scale=0.25 if k < 2 else 1.0).then_inc(qk_out, 1)
                        if k > 0:
                            act.wait_ge(rest_ready, 4 * m + k)
                            nc.scalar.activation(parts[:, u, k - 1, 1], rest[:, k - 1], ACT.Copy).then_inc(mid_ready, 1)

                pipelined(act, (root, 0), (out, 2), (turn, 1))

            @block.tensor
            def _(pe):
                pe.wait_ge(const_ready, 7)

                def turn(b, c):
                    m, u = b * CB + c, c % 2
                    pe.wait_ge(xn_ready, m + 1)
                    if late(m, 1):
                        pe.wait_ge(xnT_ready, m)
                    for t in range(TT):
                        for d in range(KD):
                            ins = pe.transpose(psT[d][:, t * P:(t + 1) * P], xn[:, u, t, d * P:(d + 1) * P], ident[:])
                    ins.then_inc(xT_ready, 1)

                def qk_products(b, c):
                    m, u = b * CB + c, c % 2
                    if isinstance(m, int) and m == 0:
                        pe.wait_ge(w_loaded, 16 * W_DMAS)
                    pe.wait_ge(xnT_ready, m + 1)
                    for k in range(4):
                        if late(m, 1):
                            pe.wait_ge(qk_out, 4 * m - 3 + k)
                        for d in range(KD):
                            ins = pe.matmul(psQK[k][:], w_sb[:, k // 2, d, (k % 2) * P:(k % 2 + 1) * P], xnT[:, u, d],
                                            start=d == 0, stop=d == KD - 1)
                        ins.then_inc(qk_ready, 1)

                def v_products(b, c):
                    m, u = b * CB + c, c % 2
                    for t in range(TT):
                        if t % 2 == 0 and late(m, 1):
                            pe.wait_ge(v_out, 2 * m - 1 + t // 2)
                        for d in range(KD):
                            ins = pe.matmul(psV[t // 2][:, t % 2], xnT[:, u, d, t * P:(t + 1) * P], w_sb[:, 2, d],
                                            start=d == 0, stop=d == KD - 1)
                        if t % 2 == 1:
                            ins.then_inc(v_ready, 1)

                pipelined(pe, (qk_products, 2), (turn, 1), (v_products, 2))

            @block.vector
            def _(dve):
                dve_alone = Alone(dve, dve_tick)

                def statistics(b, c):
                    m, u = b * CB + c, c % 2
                    dve.wait_ge(x_loaded[u], 16 * (turns(b, c) + 1))
                    for t in range(TT):
                        ins = nc.vector.bn_stats(stats[:, u, t], x_in[:, u, t])
                    ins.then_inc(stat_step, 1)
                    dve_alone.wait_ge(stat_step, 3 * m + 1)
                    for t in range(TT):
                        ins = nc.vector.bn_aggr(mv[:, u, t], stats[:, u, t])
                    ins.then_inc(stat_step, 1)
                    dve.wait_ge(stat_step, 3 * m + 2)
                    if late(m, 2):
                        dve.wait_ge(xn_ready, m - 1)
                    nc.vector.tensor_scalar(veps[:, u], mv[:, u, :, 1], EPS, None, ALU.add).then_inc(var_ready, 1)
                    nc.vector.tensor_scalar(nmean[:, u], mv[:, u, :, 0], -1.0, None, ALU.mult).then_inc(stat_step, 1)
                    dve.wait_ge(std_ready, m + 1)
                    dve.wait_ge(stat_step, 3 * m + 3)
                    nc.vector.reciprocal(rstd[:, u], std[:, u]).then_inc(rstd_ready, 1)

                def split(b, c):
                    m, u = b * CB + c, c % 2
                    if isinstance(m, int) and m == 0:
                        dve.wait_ge(w_loaded, 16 * W_DMAS)
                        dve.wait_ge(const_ready, 7)
                    for k in range(5):
                        if k < 4:
                            dve.wait_ge(hi_ready, 4 * m + k + 1)
                            if late(m, 1):
                                dve.wait_ge(low_ready, 4 * m - 3 + k)
                            nc.vector.tensor_tensor(rest[:, k], qk32[:, u, k], parts[:, u, k, 0], ALU.subtract).then_inc(rest_ready, 1)
                        if k > 0:
                            dve.wait_ge(mid_ready, 4 * m + k)
                            nc.vector.tensor_tensor(parts[:, u, k - 1, 2], rest[:, k - 1], parts[:, u, k - 1, 1], ALU.subtract).then_inc(low_ready, 1)
                    if late(m, 2):
                        dve.wait_ge(v_stored[u], 16 * QB * turns(b, c))
                    for k in range(2):
                        dve.wait_ge(v_ready, 2 * m + k + 1)
                        for t in range(2 * k, 2 * k + 2):
                            ins = nc.vector.tensor_tensor(vp[:, u, t, :, 0:DH], psV[k][:, t % 2].rearrange("p (h w) -> p h w", h=H),
                                                          bv_sb[:].rearrange("p (h w) -> p h w", h=H), ALU.add)
                        ins.then_inc(v_out, 1)

                pipelined(dve, (statistics, 0), (split, 2))


def chunk_steps(c):
    for k in range(TT):
        yield from range(c * k, c * (k + 1))
        yield TT * c + k


STEPS = [(c, j) for c in range(CB) for j in chunk_steps(c)]
FIRST = [TT * c * (c + 1) // 2 for c in range(CB + 1)]
NS = len(STEPS)
RING = 2
MW = 2 * CH
SLOTS = 2


def row_maxima():
    for t in range(KT):
        keys = (t + 1) * P
        if keys > MW // 2:
            cuts = [k * (t + 1) // -(-keys // MW) * P for k in range(-(-keys // MW) + 1)]
            for h in range(GH):
                for slot, (k0, k1) in enumerate(zip(cuts, cuts[1:])):
                    yield [(h, t, k0, k1 - k0, slot, 0)]
        else:
            together = min(GH, MW // (CH // (CH // keys)))
            for h0 in range(0, GH, together):
                yield [(h, t, 0, keys, 0, (h - h0) * (CH // (CH // keys))) for h in range(h0, h0 + together)]


MAXIMA = list(row_maxima())
NM = len(MAXIMA)
CUT = TT * (CB - 1)
SETS = [(0, CUT), (CUT, KT)]


def maximum_at(h, t):
    t0, t1 = SETS[t >= CUT]
    return GH * t0 + (t1 - t0) * h + t - t0


NA = sum(pieces[0][1] < CUT for pieces in MAXIMA)
LEAD = 12
STEP_COST = 96
Z_LAG = 3
TURN_LAG = 4
BEFORE = NA + 1
USES = NM + 2 + CB
assert USES % RING == 0


def width(c, j):
    return CH - max(0, j - TT * c) * P


def maxima_cycle(has_prev):
    rest = [("max", k, 0) for k in range(NA + LEAD if has_prev else NA, NM)]
    first = [("max", k, 1) for k in range(NA)]
    lead = [("max", k, 1) for k in range(NA, NA + LEAD)]
    return (rest + [("negate", 1, 0)] + first[:TURN_LAG] + [("turn", 1, 0)] + first[TURN_LAG:]
            + [("negate", 0, 1)] + lead[:TURN_LAG] + [("turn", 0, 1)] + lead[TURN_LAG:])


def jobs_before():
    return [("max", k, 1) for k in range(NA)] + [("negate", 0, 1), ("turn", 0, 1)]


def ring_jobs(has_prev, has_next):
    jobs = [[] for _ in range(NS)]
    if has_prev:
        jobs[Z_LAG].append(("z", CB - 1, True))
    for c in range(CB - 1):
        jobs[FIRST[c + 1] + Z_LAG].append(("z", c, False))
    room = [STEP_COST + width(*step) for step in STEPS]
    cycle = maxima_cycle(has_prev)
    cost = [sum(piece[3] for piece in MAXIMA[job[1]]) if job[0] == "max" else 256 for job in cycle]
    passed, given, spent = 0, 0, 0
    for s, w in enumerate(room):
        passed += w
        while given < len(cycle) and (spent + cost[given] / 2) * sum(room) <= passed * sum(cost):
            if has_next or not cycle[given][2]:
                jobs[s].append(cycle[given])
            spent += cost[given]
            given += 1
    return jobs


def uses(jobs):
    return [job for job in jobs if job[0] != "negate"]


def ring_base(n):
    if isinstance(n, int) and n == 0:
        return BEFORE
    return USES * n + BEFORE + LEAD - 1


LAST_USES = len(uses(job for step in ring_jobs(True, False) for job in step))


def ring_pair(n, k):
    first = {-1: 0, 0: BEFORE}.get(n, BEFORE + LEAD - 1) if isinstance(n, int) else BEFORE + LEAD - 1
    return (first + k) % RING


def uses_to_z(n, c, has_next):
    if c == CB - 1:
        n, c, has_next = n + 1, -1, True
    has_prev = not (isinstance(n, int) and n == 0)
    jobs = uses(job for step in ring_jobs(has_prev, has_next) for job in step)
    at = jobs.index(("z", CB - 1, True) if c < 0 else ("z", c, False))
    return ring_base(n) + at + 1


def load_qk(sp, qk_scr, n, buffers):
    qs, ks, loaded = buffers
    for w, dst in ((0, qs), (1, ks)):
        rows = qk_scr[w].rearrange("s b (g h d) t -> s (b g) d h t", g=QB, d=DH)
        for i, term in enumerate(TERMS):
            sp.dma_start(dst[DH * i:DH * (i + 1), :, :], rows[term[w], n]).then_inc(loaded, 16)


HT = HID // P
HB = 4
ZR = DH + 2


class OwnWeights:
    W_DMAS = 6

    def __init__(self, nc, ctx, lt_scr, xnT_scr):
        sb = lambda name, shape: ctx.enter_context(nc.sbuf_tensor(name, shape, F32))
        sem = lambda name: ctx.enter_context(nc.semaphore(name))
        self.nc, self.lt_scr, self.xnT_scr = nc, lt_scr, xnT_scr
        self.w1t = sb("w1t", [P, KD, HID])
        self.w2t = sb("w2t", [P, HT, D])
        self.next1 = sb("next1", [P, KD, HID])
        self.next2 = sb("next2", [P, HT, D])
        self.b1c = sb("b1c", [P, HT])
        self.wo = sb("wo", [ZR, D])
        self.scale_c = sb("scale_c", [P, 1])
        self.even = sb("even", [P, 2 * RANKS, D])
        self.first = sb("first", [P, KD, LORA + 4])
        self.odd = sb("odd", [P, KD, 2 * RANKS])
        self.w_loaded = sem("feed_w_loaded")
        self.scale_loaded = sem("feed_scale")
        self.first_loaded = sem("feed_first")
        self.odd_ready = sem("feed_odd_ready")
        self.outer = sem("feed_outer")
        self.next_ready = sem("feed_next_ready")
        self.eff1_ready = sem("feed_eff1_ready")
        self.eff2_ready = sem("feed_eff2_ready")

    def load(self, sp, W1T, b1, W2T, b2, WO, bO):
        sp.dma_start(self.w1t[:], W1T.rearrange("(c p) h -> p c h", p=P)).then_inc(self.w_loaded, 16)
        sp.dma_start(self.w2t[:], W2T.rearrange("(c p) o -> p c o", p=P)).then_inc(self.w_loaded, 16)
        sp.dma_start(self.b1c[:], b1.rearrange("(c p) -> p c", p=P), allow_slow_non_contiguous=True).then_inc(self.w_loaded, 16)
        sp.dma_start(self.wo[0:DH], WO).then_inc(self.w_loaded, 16)
        sp.dma_start(self.wo[DH:DH + 1], bO.rearrange("(a n) -> a n", a=1)).then_inc(self.w_loaded, 16)
        sp.dma_start(self.wo[DH + 1:DH + 2], b2.rearrange("(a n) -> a n", a=1)).then_inc(self.w_loaded, 16)

    def prepare(self, pool, pool_alone, b):
        if late(b, 1):
            pool_alone.wait_ge(self.outer, 2 * b)
        pool.dma_start(self.even[:], self.lt_scr[b * CB].rearrange("(i two) d -> two i d", two=2)[0:1].broadcast_to([P, 2 * RANKS, D])
                       ).then_inc(self.first_loaded, 16)
        pool.dma_start(self.first[:], self.xnT_scr[b * CB][:, :, 0:LORA + 4]).then_inc(self.first_loaded, 16)
        pool_alone.wait_ge(self.first_loaded, 32 * (b + 1))
        self.nc.gpsimd.tensor_scalar(self.odd[:], self.first[:, :, 2:2 + LORA:2], self.scale_c[:, 0:1], None, ALU.mult).then_inc(self.odd_ready, 1)
        pool_alone.wait_ge(self.odd_ready, b + 1)
        if late(b, 1):
            pool_alone.wait_ge(self.eff1_ready, HT * b)
        for c in range(KD):
            for i in range(RANKS):
                ins = self.nc.gpsimd.tensor_scalar(self.next1[:, c, D * i:D * (i + 1)], self.even[:, i], self.odd[:, c, i:i + 1], 1.0, ALU.mult, ALU.mult)
        ins.then_inc(self.outer, 1)
        if late(b, 1):
            pool_alone.wait_ge(self.eff2_ready, b)
        for k in range(HT):
            for i in range(RANKS):
                w = D // RANKS
                ins = self.nc.gpsimd.tensor_scalar(self.next2[:, k, w * i:w * (i + 1)], self.even[:, RANKS + i, k // KD::RANKS],
                                              self.odd[:, k % KD, RANKS + i:RANKS + i + 1], 1.0, ALU.mult, ALU.mult)
        ins.then_inc(self.outer, 1)
        pool_alone.wait_ge(self.outer, 2 * b + 2)
        self.nc.gpsimd.tensor_tensor(self.next1[:], self.next1[:], self.w1t[:], ALU.add).then_inc(self.next_ready, 1)
        self.nc.gpsimd.tensor_tensor(self.next2[:], self.next2[:], self.w2t[:], ALU.add).then_inc(self.next_ready, 1)


def attend(nc, const, qk_scr, v_scr, m_scr, zn_scr, group0, stored, zn_stored, own, weights, scale):
    ident, mask = const["ident"], const["mask"]
    with ExitStack() as ctx:
        sb = lambda name, shape, dt=F32: ctx.enter_context(nc.sbuf_tensor(name, shape, dt))
        sem = lambda name: ctx.enter_context(nc.semaphore(name))
        mx = sb("mx", [P, GH * KT, SLOTS])
        negm = sb("negm", [P, P])
        mrest = sb("mrest", [GH * KT, P])
        mparts = sb("mparts", [GH * KT, PARTS, P], BF16)
        qs0, ks0, qk_loaded0 = group0
        qs = [qs0] + [sb(f"qs{u}", [KMAX, GH, S], BF16) for u in range(1, 3)]
        ks = [ks0] + [sb(f"ks{u}", [KMAX, GH, S], BF16) for u in range(1, 3)]
        vq = [sb(f"vq{u}", [P, KT, GH, VW]) for u in range(3)]
        pr = [[sb(f"pr{p}{v}", [P, 2, CH]) for v in range(2)] for p in range(2)]
        zt = [sb(f"zt{v}", [P, CH]) for v in range(2)]
        rl = sb("rl", [P, TT, GH])
        zn = [sb(f"zn{v}", [P, TT, GH, DH]) for v in range(2)]
        sc = [ctx.enter_context(nc.psum_tensor(f"sc{k}", [P, CH], F32)) for k in range(3)]
        ring = [ctx.enter_context(nc.psum_tensor(f"ring{k}", [P, MW], F32)) for k in range(RING)]
        pv = ctx.enter_context(nc.psum_tensor("pv", [P, CH], F32))

        qk_loaded = [qk_loaded0] + [sem(f"qk_loaded{u}") for u in range(1, 3)]
        v_loaded = [sem(f"v_loaded{u}") for u in range(3)]
        set_up = sem("set_up")
        ones_landed = sem("ones_landed")
        sc_ready = sem("sc_ready")
        exp_done = sem("exp_done")
        masked = sem("masked")
        pv_done = sem("pv_done")
        zt_done = sem("zt_done")
        ring_ready = sem("ring_ready")
        ring_done = sem("ring_done")
        negm_ready = sem("negm_ready")
        m_step = sem("m_step")
        m_stored = sem("m_stored")
        m_landed = sem("m_landed")
        rl_ready = sem("rl_ready")
        QKD = 16 * 2 * len(TERMS)
        DIAG = 2 * TT * CB

        def groups(eng, group):
            group(0, 0, 0, False, True)
            looped = (QUADS - 2) // 3
            with eng.Fori(0, looped) as i:
                group(3 * i + 1, i, 1, True, True)
                group(3 * i + 2, i, 2, True, True)
                group(3 * i + 3, i + 1, 0, True, True)
            for n in range(3 * looped + 1, QUADS):
                group(n, n // 3, n % 3, True, n + 1 < QUADS)

        def bank(n3, s, h):
            return (n3 * GH * NS + GH * s + h) % 3

        pool_tick, dve_tick, sp_tick = sem("pool_tick2"), sem("dve_tick2"), sem("sp_tick2")

        with nc.Block() as block:
            @block.sync
            def _(sp):
                sp_alone = Alone(sp, sp_tick)
                def load_v(n, u):
                    sp.dma_start(vq[u][:].rearrange("p j h w -> p j (h w)"),
                                 v_scr.rearrange("b g p j w -> (b g) p j w")[n]).then_inc(v_loaded[u], 16)

                def put_maxima(done, which, n, u):
                    sp_alone.wait_ge(ring_done, done)
                    t0, t1 = SETS[which]
                    there = m_scr[n, :, GH * t0:GH * t1, :]
                    sp.dma_start(there.rearrange("s r p -> r s p"), mparts[GH * t0:GH * t1]).then_inc(m_stored, 16)
                    sp.wait_ge(m_stored, 16 * (2 * n + which + 1))
                    sp.dma_start(qs[u][KROWS:KMAX, :, t0 * P:t1 * P], there.rearrange("s (h t) p -> s h (t p)", h=GH)).then_inc(m_landed, 16)

                def store_z(n, c, done):
                    sp_alone.wait_ge(ring_done, done)
                    sp.dma_start(zn_scr[n, c], zn[c % 2][:].rearrange("p t h d -> p t (h d)")).then_inc(zn_stored[c % 2], 16)

                def group(n, r, u, has_prev, has_next):
                    if has_prev:
                        sp.wait_ge(pv_done, NS * n)
                    if not isinstance(n, int) or n + 2 < QUADS:
                        load_qk(sp, qk_scr, n + 2, (qs[(u + 2) % 3], ks[(u + 2) % 3], qk_loaded[(u + 2) % 3]))
                        load_v(n + 2, (u + 2) % 3)
                    done = ring_base(n)
                    for jobs in ring_jobs(has_prev, has_next):
                        for job in uses(jobs):
                            done = done + 1
                            if job[0] == "z":
                                store_z(n - 1 if job[2] else n, job[1], done)
                            if job[0] == "turn":
                                put_maxima(done, job[1], n + job[2], (u + job[2]) % 3)
                    if not has_next:
                        store_z(n, CB - 1, done + 1)

                for per_chunk, sems in zip((1, 1, 4, QB), stored):
                    for u in range(2):
                        sp.wait_ge(sems[u], 16 * per_chunk * NCH // 2)
                load_v(0, 0)
                load_qk(sp, qk_scr, 1, (qs[1], ks[1], qk_loaded[1]))
                load_v(1, 1)
                for u in range(3):
                    for s in range(PARTS):
                        sp.dma_start(ks[u][KROWS + s:KROWS + s + 1, :, :], const["ones"][:]).then_inc(ones_landed, 16)
                own.load(sp, *weights)
                put_maxima(BEFORE, 0, 0, 0)
                groups(sp, group)

            @block.gpsimd
            def _(pool):
                pool_alone = Alone(pool, pool_tick)
                def group(n, r, u, has_prev, has_next):
                    for s, (c, j) in enumerate(STEPS):
                        q0 = CH - width(c, j)
                        if j < TT * c:
                            continue
                        for p in range(2):
                            pool_alone.wait_ge(exp_done, GH * (NS * n + s) + 2 * p + 2)
                            tile = pr[p][s % 2][:, :, q0:q0 + P]
                            nc.gpsimd.affine_select(out=tile, in_=tile, compare_op=ALU.is_ge, fill=0.0, base=0,
                                                    pattern=[[0, 2], [1, P]], channel_multiplier=-1).then_inc(masked, 1)

                pool.dma_start(own.scale_c[:], scale.broadcast_to([P, 1])).then_inc(own.scale_loaded, 16)
                pool.wait_ge(own.scale_loaded, 16)
                pool.wait_ge(own.w_loaded, 16 * own.W_DMAS)
                own.prepare(pool, pool_alone, 0)
                groups(pool, group)

            @block.scalar
            def _(act):
                def z_out(n, c, has_next):
                    g = CB * n + c
                    act.wait_ge(pv_done, NS * n + FIRST[c + 1])
                    if late(g, 2):
                        act.wait_ge(ring_done, uses_to_z(n, c - 2, has_next) if c >= 2 else uses_to_z(n - 1, c + CB - 2, True))
                    nc.scalar.activation(zt[c % 2][:], pv[:], ACT.Copy).then_inc(zt_done, 1)

                def group(n, r, u, has_prev, has_next):
                    for s, (c, j) in enumerate(STEPS):
                        q0 = CH - width(c, j)
                        for h in range(GH):
                            act.wait_ge(sc_ready, GH * (NS * n + s) + h + 1)
                            if h == 0 and (has_prev or s >= 2):
                                act.wait_ge(pv_done, NS * n + s - 1)
                            nc.scalar.activation(pr[h // 2][s % 2][:, h % 2, q0:], sc[bank(u, s, h)][:, q0:], ACT.Exp).then_inc(exp_done, 1)
                        if s == FIRST[c] and c > 0:
                            z_out(n, c - 1, has_next)
                        if s == 0 and has_prev:
                            z_out(n - 1, CB - 1, True)

                groups(act, group)
                z_out(QUADS - 1, CB - 1, False)

            @block.tensor
            def _(pe):
                def ring_job(job, base, k, n, of):
                    if k >= RING:
                        pe.wait_ge(ring_done, base + k - RING + 1)
                    elif not (isinstance(base, int) and base == 0):
                        pe.wait_ge(ring_done, base)
                    pair = ring[ring_pair(n, k)]
                    if job[0] == "max":
                        for h, t, k0, keys, _, at in MAXIMA[job[1]]:
                            for k1 in range(0, keys, CH):
                                w = min(CH, keys - k1)
                                ins = pe.matmul(pair[:, at + k1:at + k1 + w], qs[of][0:KROWS, h, t * P:(t + 1) * P],
                                                ks[of][0:KROWS, h, k0 + k1:k0 + k1 + w], start=True, stop=True)
                        ins.then_inc(ring_ready, 1)
                    if job[0] == "turn":
                        pe.wait_ge(negm_ready, 2 * (n + job[2]) + job[1] + 1)
                        pe.transpose(pair[:, 0:P], negm[:], ident[:]).then_inc(ring_ready, 1)
                    if job[0] == "z":
                        c = job[1]
                        pe.wait_ge(zt_done, CB * (n - 1 if job[2] else n) + c + 1)
                        for t in range(TT):
                            ins = pe.transpose(pair[:, t * P:(t + 1) * P], zt[c % 2][:, t * P:(t + 1) * P], ident[:])
                        ins.then_inc(ring_ready, 1)

                def scores(n, u, s, h):
                    c, j = STEPS[s]
                    q0 = CH - width(c, j)
                    if s > 0 or h > 2 or not (isinstance(n, int) and n == 0):
                        pe.wait_ge(exp_done, GH * (NS * n + s) + h - 2)
                    pe.matmul(sc[bank(u, s, h)][:, q0:], ks[u][:, h, j * P:(j + 1) * P], qs[u][:, h, c * CH + q0:(c + 1) * CH],
                              start=True, stop=True).then_inc(sc_ready, 1)

                def values(n, r, u, s):
                    c, j = STEPS[s]
                    q0 = CH - width(c, j)
                    if s == FIRST[c]:
                        pe.wait_ge(v_loaded[u], 16 * (r + 1))
                        if c > 0 or not (isinstance(n, int) and n == 0):
                            pe.wait_ge(zt_done, CB * n + c)
                    if j >= TT * c:
                        pe.wait_ge(masked, DIAG * n + 2 * j + 2)
                    else:
                        pe.wait_ge(exp_done, GH * (NS * n + s + 1))
                    for h in range(GH):
                        ins = pe.matmul(pv[VW * h:VW * (h + 1), q0:], vq[u][:, j, h], pr[h // 2][s % 2][:, h % 2, q0:],
                                        start=s == FIRST[c], stop=s + 1 == FIRST[c + 1])
                    ins.then_inc(pv_done, 1)

                def group(n, r, u, has_prev, has_next):
                    base, k = ring_base(n), 0
                    pe.wait_ge(m_landed, 16 * (2 * n + 1))
                    for s, jobs in enumerate(ring_jobs(has_prev, has_next)):
                        if s == FIRST[CB - 1]:
                            pe.wait_ge(m_landed, 16 * (2 * n + 2))
                        if ("max", 0, 1) in jobs:
                            pe.wait_ge(qk_loaded[(u + 1) % 3], QKD * (r + (u + 1) // 3 + 1))
                        jobs = uses(jobs)
                        for part in range(3):
                            if part < 2:
                                scores(n, u, s, 2 * part)
                                scores(n, u, s, 2 * part + 1)
                            elif s > 0:
                                values(n, r, u, s - 1)
                            elif has_prev:
                                values(n - 1, r if u else r - 1, (u + 2) % 3, NS - 1)
                            for job in jobs[(part * len(jobs) + 2) // 3:((part + 1) * len(jobs) + 2) // 3]:
                                ring_job(job, base, k, n, None if job[0] == "z" else (u + job[2]) % 3)
                                k += 1

                pe.wait_ge(qk_loaded[0], QKD)
                for k, job in enumerate(uses(jobs_before())):
                    ring_job(job, 0, k, -1, 0)
                pe.wait_ge(ones_landed, 16 * 3 * PARTS)
                groups(pe, group)
                values(QUADS - 1, (QUADS - 1) // 3, (QUADS - 1) % 3, NS - 1)
                ring_job(("z", CB - 1, False), ring_base(QUADS - 1), LAST_USES, QUADS - 1, None)

            @block.vector
            def _(dve):
                dve_alone = Alone(dve, dve_tick)
                def negate(job, done, n):
                    dve.wait_ge(ring_done, done)
                    nc.vector.tensor_reduce(negm[:, 0:GH * KT], mx[:], AX.X, ALU.max,
                                            negate=True).then_inc(negm_ready, 1)
                    dve_alone.wait_ge(negm_ready, 2 * (n + job[2]) + job[1] + 1)

                def ring_job(job, done, n, bank):
                    if job[0] == "z":
                        dve.wait_ge(ring_done, done)
                    dve_alone.wait_ge(ring_ready, done + 1)
                    if job[0] == "max":
                        for h, t, k0, keys, slot, at in MAXIMA[job[1]]:
                            to = mx[:, maximum_at(h, t), slot:slot + 1]
                            piece = bank[:, at:at + keys]
                            if k0 + keys < (t + 1) * P:
                                ins = nc.vector.tensor_reduce(to, piece, AX.X, ALU.max)
                            else:
                                ins = nc.vector.tensor_tensor_reduce(out=piece, in0=piece, in1=mask[:, MW - keys:MW], scale=1.0,
                                                                     scalar=NEG, op0=ALU.add, op1=ALU.max, accum_out=to)
                        ins.then_inc(ring_done, 1)
                    if job[0] == "turn":
                        sets = 2 * (n + job[2]) + job[1]
                        if not (isinstance(sets, int) and sets == 0):
                            dve.wait_ge(m_stored, 16 * sets)
                        rows = bank[0:GH * KT, 0:P]
                        base = 3 * sets
                        nc.vector.tensor_copy(mparts[:, 0], rows).then_inc(m_step, 1)
                        dve.wait_ge(m_step, base + 1)
                        nc.vector.tensor_tensor(mrest[:], rows, mparts[:, 0], ALU.subtract).then_inc(m_step, 1)
                        dve.wait_ge(m_step, base + 2)
                        nc.vector.tensor_copy(mparts[:, 1], mrest[:]).then_inc(m_step, 1)
                        dve.wait_ge(m_step, base + 3)
                        nc.vector.tensor_tensor(mparts[:, 2], mrest[:], mparts[:, 1], ALU.subtract).then_inc(ring_done, 1)
                    if job[0] == "z":
                        nn, c = (n - 1 if job[2] else n), job[1]
                        g = CB * nn + c
                        z = bank[:, 0:CH].rearrange("p (t h w) -> p t h w", t=TT, h=GH)
                        nc.vector.reciprocal(rl[:], z[:, :, :, DH]).then_inc(rl_ready, 1)
                        dve.wait_ge(rl_ready, g + 1)
                        if late(g, 2):
                            dve.wait_ge(zn_stored[c % 2], 16 * turns(nn, c))
                        nc.vector.tensor_tensor(zn[c % 2][:], z[:, :, :, 0:DH], rl[:].unsqueeze(3).broadcast_to([P, TT, GH, DH]),
                                                ALU.mult).then_inc(ring_done, 1)

                def run_jobs(jobs, base, n):
                    k = 0
                    for job in jobs:
                        if job[0] == "negate":
                            negate(job, base + k, n)
                        else:
                            ring_job(job, base + k, n, ring[ring_pair(n, k)])
                            k += 1

                def group(n, r, u, has_prev, has_next):
                    run_jobs([job for jobs in ring_jobs(has_prev, has_next) for job in jobs], ring_base(n), n)

                nc.vector.memset(mx[:], NEG).then_inc(set_up, 1)
                nc.vector.memset(negm[:], 0.0).then_inc(set_up, 1)

                dve.wait_ge(set_up, 2)
                run_jobs(jobs_before(), 0, -1)
                groups(dve, group)
                ring_job(("z", CB - 1, False), ring_base(QUADS - 1) + LAST_USES, QUADS - 1, ring[ring_pair(QUADS - 1, LAST_USES)])


def feed(nc, const, x, own, xnT_scr, zn_scr, zn_stored, out):
    ident = const["ident"]
    with ExitStack() as ctx:
        sb = lambda name, shape, dt=F32: ctx.enter_context(nc.sbuf_tensor(name, shape, dt))
        sem = lambda name: ctx.enter_context(nc.semaphore(name))
        eff1 = sb("eff1", [P, KD, HID])
        eff2 = sb("eff2", [P, HT, D])
        xc = [sb(f"xc{u}", [P, KD, CH]) for u in range(2)]
        x_res = [sb(f"x_res{u}", [P, TT, D]) for u in range(2)]
        zn_in = [sb(f"zn_in{u}", [P, QB, TT, GH * DH]) for u in range(2)]
        zs = [sb(f"zs{u}", [P, TT, ZR]) for u in range(2)]
        zT = [sb(f"zT{u}", [ZR, CH]) for u in range(2)]
        g = [sb(f"g{u}", [P, HT, CH]) for u in range(2)]
        y = [sb(f"y{u}", [P, TT, D]) for u in range(2)]
        ps_h = [ctx.enter_context(nc.psum_tensor(f"ps_h{k}", [P, CH], F32)) for k in range(HB)]
        ps_y = [ctx.enter_context(nc.psum_tensor(f"ps_y{k}", [P, CH], F32)) for k in range(2)]
        ps_z = ctx.enter_context(nc.psum_tensor("ps_z", [P, CH], F32))

        ones_set = sem("feed_ones_set")
        xc_loaded = [sem(f"feed_xc_loaded{u}") for u in range(2)]
        x_loaded = [sem(f"feed_x_loaded{u}") for u in range(2)]
        z_loaded = [sem(f"feed_z_loaded{u}") for u in range(2)]
        zs_ready = sem("feed_zs_ready")
        z_turned = sem("feed_z_turned")
        zT_ready = sem("feed_zT_ready")
        h_ready = sem("feed_h_ready")
        g_ready = sem("feed_g_ready")
        y_made = sem("feed_y_made")
        y_ready = sem("feed_y_ready")
        y_stored = [sem(f"feed_y_stored{u}") for u in range(2)]
        pool_tick = sem("pool_tick3")

        with nc.Block() as block:
            @block.sync
            def _(sp):
                def load(b, c):
                    m, u = b * CB + c, c % 2
                    if late(m, 2):
                        sp.wait_ge(h_ready, HT * (m - 1))
                    sp.dma_start(xc[u][:], xnT_scr[m]).then_inc(xc_loaded[u], 16)
                    if isinstance(m, int) and m == 0:
                        for v in range(2):
                            sp.wait_ge(zn_stored[v], 16 * CB * QUADS // 2)
                    if late(m, 2):
                        sp.wait_ge(zs_ready, m - 1)
                    sp.dma_start(zn_in[u][:].rearrange("p q t w -> p q (t w)"),
                                 zn_scr.rearrange("(b q) c p t w -> b c p q (t w)", q=QB)[b, c]).then_inc(z_loaded[u], 16)
                    if late(m, 2):
                        sp.wait_ge(y_ready, TT * (m - 1))
                    sp.dma_start(x_res[u][:], x[b, c * CH:(c + 1) * CH, :].rearrange("(t p) d -> p t d", p=P)).then_inc(x_loaded[u], 16)

                def store(b, c):
                    m, u = b * CB + c, c % 2
                    sp.wait_ge(y_ready, TT * (m + 1))
                    sp.dma_start(out[b, c * CH:(c + 1) * CH, :].rearrange("(t p) d -> p t d", p=P), y[u][:]).then_inc(y_stored[u], 16)

                pipelined(sp, (load, 0), (store, 2))
                for u in range(2):
                    sp.wait_ge(y_stored[u], 16 * NCH // 2)

            @block.gpsimd
            def _(pool):
                pool_alone = Alone(pool, pool_tick)
                for u in range(2):
                    nc.gpsimd.memset(zs[u][:, :, DH:DH + 1], float(H)).then_inc(ones_set, 1)
                    nc.gpsimd.memset(zs[u][:, :, DH + 1:DH + 2], 1.0).then_inc(ones_set, 1)
                with pool.Fori(1, B) as b:
                    own.prepare(pool, pool_alone, b)

            @block.scalar
            def _(act):
                def gelu(b, c):
                    m, u = b * CB + c, c % 2
                    if late(m, 2):
                        act.wait_ge(y_made, TT * (m - 1))
                    for k in range(HT):
                        act.wait_ge(h_ready, HT * m + k + 1)
                        nc.scalar.activation(g[u][:, k], ps_h[k % HB][:], ACT.Gelu, bias=own.b1c[:, k:k + 1]).then_inc(g_ready, 1)
                    act.wait_ge(z_turned, m + 1)
                    nc.scalar.activation(zT[u][:], ps_z[0:ZR], ACT.Identity).then_inc(zT_ready, 1)

                pipelined(act, (gelu, 0))

            @block.tensor
            def _(pe):
                def hidden(b, c):
                    m, u = b * CB + c, c % 2
                    pe.wait_ge(xc_loaded[u], 16 * (turns(b, c) + 1))
                    for k in range(HT):
                        if late(m, 1) or k >= HB:
                            pe.wait_ge(g_ready, HT * m + k - HB + 1)
                        if c == 0:
                            pe.wait_ge(own.eff1_ready, HT * b + k + 1)
                        for d in range(KD):
                            ins = pe.matmul(ps_h[k % HB][:], eff1[:, d, k * P:(k + 1) * P], xc[u][:, d], start=d == 0, stop=d == KD - 1)
                        ins.then_inc(h_ready, 1)
                    pe.wait_ge(zs_ready, m + 1)
                    if late(m, 1):
                        pe.wait_ge(zT_ready, m)
                    for t in range(TT):
                        ins = pe.transpose(ps_z[0:ZR, t * P:(t + 1) * P], zs[u][:, t], ident[:])
                    ins.then_inc(z_turned, 1)

                def outputs(b, c):
                    m, u = b * CB + c, c % 2
                    pe.wait_ge(g_ready, HT * (m + 1))
                    pe.wait_ge(zT_ready, m + 1)
                    if c == 0:
                        pe.wait_ge(own.eff2_ready, b + 1)
                    for t in range(TT):
                        if late(m, 1) or t >= 2:
                            pe.wait_ge(y_ready, TT * m + t - 1)
                        to = ps_y[t % 2][:, 0:D]
                        pe.matmul(to, zT[u][:, t * P:(t + 1) * P], own.wo[:], start=True, stop=False)
                        for k in range(HT):
                            ins = pe.matmul(to, g[u][:, k, t * P:(t + 1) * P], eff2[:, k], start=False, stop=k == HT - 1)
                        ins.then_inc(y_made, 1)

                pipelined(pe, (hidden, 0), (outputs, 1))

            @block.vector
            def _(dve):
                dve.wait_ge(ones_set, 4)

                def take_over(b, c):
                    m = b * CB + c
                    if c == 0:
                        dve.wait_ge(own.next_ready, 2 * b + 2)
                        for k in range(HT):
                            if late(b, 1):
                                dve.wait_ge(h_ready, HT * (m - 1) + k + 1)
                            tile = slice(k * P, (k + 1) * P)
                            nc.vector.tensor_copy(eff1[:, :, tile], own.next1[:, :, tile]).then_inc(own.eff1_ready, 1)
                    if c == 1:
                        if late(b, 1):
                            dve.wait_ge(y_made, TT * (m - 1))
                        nc.vector.tensor_copy(eff2[:], own.next2[:]).then_inc(own.eff2_ready, 1)

                def gather(b, c):
                    m, u = b * CB + c, c % 2
                    if isinstance(m, int) and m == 0:
                        take_over(b, c)
                    dve.wait_ge(z_loaded[u], 16 * (turns(b, c) + 1))
                    if late(m, 2):
                        dve.wait_ge(z_turned, m - 1)
                    for t in range(TT):
                        ins = nc.vector.tensor_reduce(zs[u][:, t, 0:DH], zn_in[u][:, :, t].rearrange("p q (h d) -> p d q h", d=DH), AX.XY, ALU.add)
                    ins.then_inc(zs_ready, 1)
                    if not isinstance(m, int) or m > 0:
                        take_over(b, c)

                def finish(b, c):
                    m, u = b * CB + c, c % 2
                    dve.wait_ge(x_loaded[u], 16 * (turns(b, c) + 1))
                    if late(m, 2):
                        dve.wait_ge(y_stored[u], 16 * turns(b, c))
                    for t in range(TT):
                        dve.wait_ge(y_made, TT * m + t + 1)
                        nc.vector.tensor_tensor(y[u][:, t], ps_y[t % 2][:, 0:D], x_res[u][:, t], ALU.add).then_inc(y_ready, 1)

                pipelined(dve, (gather, 0), (finish, 1))


def program(nc, x, WQ, bQ, WK, bK, WV, bV, WO, bO, W1T, b1, W2T, b2, scale, out):
    scr = lambda name, shape, dt=F32: nc.dram_tensor(name, shape, dt, kind="Internal").ap()
    qk_scr = scr("qk_scr", [2, PARTS, B, D, S], BF16)
    v_scr = scr("v_scr", [B, QB, P, KT, GH * VW])
    xnT_scr = scr("xnT_scr", [NCH, P, KD, CH])
    lt_scr = scr("lt_scr", [NCH, LORA, D])
    m_scr = scr("m_scr", [QUADS, PARTS, GH * KT, P], BF16)
    zn_scr = scr("zn_scr", [QUADS, CB, P, TT, GH * DH])
    with ExitStack() as ctx:
        const = {
            "ident": ctx.enter_context(nc.sbuf_tensor("ident", [P, P], F32)),
            "ones": ctx.enter_context(nc.sbuf_tensor("ones", [GH * KT, P], BF16)),
            "mask": ctx.enter_context(nc.sbuf_tensor("mask", [P, 2 * CH], F32)),
        }
        stored = [[ctx.enter_context(nc.semaphore(f"{name}_stored{u}")) for u in range(2)] for name in ("lt", "xnT", "qk", "v")]
        zn_stored = [ctx.enter_context(nc.semaphore(f"zn_stored{u}")) for u in range(2)]
        group0 = (ctx.enter_context(nc.sbuf_tensor("qs0", [KMAX, GH, S], BF16)),
                  ctx.enter_context(nc.sbuf_tensor("ks0", [KMAX, GH, S], BF16)),
                  ctx.enter_context(nc.semaphore("qk_loaded0")))
        project(nc, const, x, WQ, bQ, WK, bK, WV, bV, qk_scr, v_scr, xnT_scr, lt_scr, group0, stored)
        own = OwnWeights(nc, ctx, lt_scr, xnT_scr)
        attend(nc, const, qk_scr, v_scr, m_scr, zn_scr, group0, stored, zn_stored, own, (W1T, b1, W2T, b2, WO, bO), scale)
        feed(nc, const, x, own, xnT_scr, zn_scr, zn_stored, out)


def kernel(**inputs):
    import numpy as np
    import concourse.bacc as bacc
    from concourse.bass_utils import run_bass_kernel_spmd

    a = {k.removeprefix("L0_attn_").removeprefix("L0_ffn_"): np.asarray(v) for k, v in inputs.items()}
    arrays = {
        "x": a["x"], "WQ": a["WQ"], "bQ": a["bQ"], "WK": a["WK"], "bK": a["bK"], "WV": a["WV"], "bV": a["bV"],
        "WO": a["WO"], "bO": a["bO"], "W1T": a["W1"].T, "b1": a["b1"], "W2T": a["W2"].T, "b2": a["b2"],
        "scale": a["scale"].reshape(1, 1),
    }
    nc = bacc.Bacc("TRN2", target_bir_lowering=False, num_devices=1)
    given, aps = {}, []
    for name, v in arrays.items():
        v = np.ascontiguousarray(v)
        given[f"in_{name}"] = v
        aps.append(nc.dram_tensor(f"in_{name}", v.shape, mybir.dt.from_np(v.dtype), kind="ExternalInput").ap())
    out = nc.dram_tensor("out_y", (B, S, D), F32, kind="ExternalOutput").ap()
    program(nc, *aps, out)
    r = run_bass_kernel_spmd(nc, [given], core_ids=[0])
    return r.results[0]["out_y"]
```
